# Optimizing a Trainium2 kernel written in Bass

```python
import numpy as np
import jax
import jax.numpy as jnp

def _softmax(x, axis=-1):
    return jax.nn.softmax(x, axis=axis)

def _gelu(x):
    return jax.nn.gelu(x, approximate=True)

def _silu(x):
    return jax.nn.silu(x)

def _sigmoid(x):
    return jax.nn.sigmoid(x)

def _layernorm(x, axis=-1, eps=1e-05):
    m = jnp.mean(x, axis=axis, keepdims=True)
    v = jnp.var(x, axis=axis, keepdims=True)
    return (x - m) / jnp.sqrt(v + eps)

def _scatter_add(tgt, idx, src, axis=0):
    return tgt.at[idx].add(src)

def _segment_sum(src, seg, n):
    return jax.ops.segment_sum(src, seg, n)
kernel_name = 'mk_xattn_ffn_d1_seqx_r8_581a45'

def setup_inputs(seed: int=0):
    np.random.seed(seed)
    _w = jnp.asarray

    def _rec_inputs():
        import jax
        import jax.numpy as jnp
        _rk = jax.random.key(seed)
        x = -0.000125 + 0.9999 * jax.random.normal(jax.random.fold_in(_rk, 1), (16, 128, 256), jnp.float32)
        _lenS = 128 - jax.random.randint(jax.random.fold_in(_rk, 7), (16,), 0, max(1, 128 // 4) + 1, jnp.int32)
        _lenS2 = 128 - jax.random.randint(jax.random.fold_in(_rk, 8), (16,), 0, max(1, 128 // 4) + 1, jnp.int32)
        _ctx_2048P = jax.random.normal(jax.random.fold_in(_rk, 11), (16, 16, 256), jnp.float32)
        _ctx_2048c = jax.random.dirichlet(jax.random.fold_in(_rk, 511), 0.3 * jnp.ones((16,), jnp.float32), (16, 128))
        _ctx_2048t = jnp.einsum('bsk,bkd->bsd', _ctx_2048c, _ctx_2048P)
        _ctx_2048t = _ctx_2048t * jax.lax.rsqrt(jnp.mean(jnp.square(_ctx_2048t)) + 1e-12) * 0.953939
        ctx_2048 = -1.52775e-05 + 0.999936 * (_ctx_2048t + 0.3 * jax.random.normal(jax.random.fold_in(_rk, 611), (16, 128, 256), jnp.float32))
        return (x, ctx_2048)
    x, ctx_2048 = _rec_inputs()

    def _L0_xattn_setup():
        import jax, jax.numpy as jnp
        import numpy as np
        B, DIM1, DIM2, LATENT, T = (16, 128, 128, 64, 256)
        LN_EPS = 1e-05
        key = jax.random.key(seed)
        ks = jax.random.split(key, 8)

        def xavier(k, shape):
            fan_out, fan_in = shape
            std = float(np.sqrt(2.0 / (fan_in + fan_out)))
            return jax.random.normal(k, shape, dtype=jnp.float32) * std
        return {'input1': jax.random.normal(ks[0], (B, DIM1, T), dtype=jnp.float32), 'input2': jax.random.normal(ks[1], (B, DIM2, T), dtype=jnp.float32), 'theta_w': xavier(ks[2], (LATENT, DIM2)), 'theta_b': jnp.zeros((LATENT,), jnp.float32), 'phi_w': xavier(ks[3], (LATENT, DIM1)), 'phi_b': jnp.zeros((LATENT,), jnp.float32), 'g_w': xavier(ks[4], (LATENT, DIM1)), 'g_b': jnp.zeros((LATENT,), jnp.float32), 'ln_gamma': jnp.ones((LATENT, T), jnp.float32), 'ln_beta': jnp.zeros((LATENT, T), jnp.float32), 'out_w': xavier(ks[5], (DIM2, LATENT)), 'out_b': jnp.zeros((DIM2,), jnp.float32)}
    _L0_xattn_all = _L0_xattn_setup()
    _L0_xattn_in = {k: v for k, v in _L0_xattn_all.items() if k in ('theta_w', 'theta_b', 'phi_w', 'phi_b', 'g_w', 'g_b', 'ln_gamma', 'ln_beta', 'out_w', 'out_b')}
    del _L0_xattn_all

    def _L0_ffn_setup():
        import jax, jax.numpy as jnp
        import numpy as np
        DIM = 256
        INTER = 176
        E = 16
        TOPK = 4
        G = 4
        TOPK_G = 2
        N_SHARED = 2
        SHARED_INTER = N_SHARED * INTER
        ROUTE_SCALE = 1.0

        def _moe_forward(x, Wg, W1, W3, W2, Ws1, Ws3, Ws2):
            B, S, D = x.shape
            xt = x.reshape(-1, D)
            T = xt.shape[0]
            scores = jax.nn.softmax(xt @ Wg.T, axis=-1)
            sg = scores.reshape(T, G, E // G)
            group_scores = sg.max(axis=-1)
            gidx = jax.lax.top_k(group_scores, TOPK_G)[1]
            gmask = jax.nn.one_hot(gidx, G, dtype=jnp.float32).sum(axis=1) > 0
            masked = jnp.where(gmask[:, :, None], sg, -jnp.inf).reshape(T, E)
            topi = jax.lax.top_k(masked, TOPK)[1]
            weights = jnp.take_along_axis(scores, topi, axis=1) * ROUTE_SCALE
            combine = jnp.zeros((T, E), xt.dtype).at[jnp.arange(T)[:, None], topi].add(weights)
            h = jax.nn.silu(jnp.einsum('td,eid->eti', xt, W1)) * jnp.einsum('td,eid->eti', xt, W3)
            expert_out = jnp.einsum('eti,edi->etd', h, W2)
            y = jnp.einsum('etd,te->td', expert_out, combine)
            z = jax.nn.silu(xt @ Ws1.T) * (xt @ Ws3.T) @ Ws2.T
            return (y + z).reshape(B, S, D)
        key = jax.random.key(seed)
        ks = jax.random.split(key, 8)
        s = 0.02
        x = jax.random.normal(ks[0], (1, 256, DIM), dtype=jnp.float32)
        Wg = jax.random.normal(ks[1], (E, DIM), dtype=jnp.float32) * s
        W1 = jax.random.normal(ks[2], (E, INTER, DIM), dtype=jnp.float32) * s
        W3 = jax.random.normal(ks[3], (E, INTER, DIM), dtype=jnp.float32) * s
        W2 = jax.random.normal(ks[4], (E, DIM, INTER), dtype=jnp.float32) * s
        Ws1 = jax.random.normal(ks[5], (SHARED_INTER, DIM), dtype=jnp.float32) * s
        Ws3 = jax.random.normal(ks[6], (SHARED_INTER, DIM), dtype=jnp.float32) * s
        Ws2 = jax.random.normal(ks[7], (DIM, SHARED_INTER), dtype=jnp.float32) * s
        return {'x': x, 'Wg': Wg, 'W1': W1, 'W3': W3, 'W2': W2, 'Ws1': Ws1, 'Ws3': Ws3, 'Ws2': Ws2}
    _L0_ffn_all = _L0_ffn_setup()
    _L0_ffn_in = {k: v for k, v in _L0_ffn_all.items() if k in ('Wg', 'W1', 'W3', 'W2', 'Ws1', 'Ws3', 'Ws2')}
    del _L0_ffn_all
    return {'x': x, 'ctx_2048': ctx_2048, 'L0_xattn_theta_w': _L0_xattn_in['theta_w'], 'L0_xattn_theta_b': _L0_xattn_in['theta_b'], 'L0_xattn_phi_w': _L0_xattn_in['phi_w'], 'L0_xattn_phi_b': _L0_xattn_in['phi_b'], 'L0_xattn_g_w': _L0_xattn_in['g_w'], 'L0_xattn_g_b': _L0_xattn_in['g_b'], 'L0_xattn_ln_gamma': _L0_xattn_in['ln_gamma'], 'L0_xattn_ln_beta': _L0_xattn_in['ln_beta'], 'L0_xattn_out_w': _L0_xattn_in['out_w'], 'L0_xattn_out_b': _L0_xattn_in['out_b'], 'L0_ffn_Wg': _L0_ffn_in['Wg'], 'L0_ffn_W1': _L0_ffn_in['W1'], 'L0_ffn_W3': _L0_ffn_in['W3'], 'L0_ffn_W2': _L0_ffn_in['W2'], 'L0_ffn_Ws1': _L0_ffn_in['Ws1'], 'L0_ffn_Ws3': _L0_ffn_in['Ws3'], 'L0_ffn_Ws2': _L0_ffn_in['Ws2']}

def reference(x, ctx_2048, L0_xattn_theta_w, L0_xattn_theta_b, L0_xattn_phi_w, L0_xattn_phi_b, L0_xattn_g_w, L0_xattn_g_b, L0_xattn_ln_gamma, L0_xattn_ln_beta, L0_xattn_out_w, L0_xattn_out_b, L0_ffn_Wg, L0_ffn_W1, L0_ffn_W3, L0_ffn_W2, L0_ffn_Ws1, L0_ffn_Ws3, L0_ffn_Ws2):
    import jax
    import jax.numpy as jnp

    def _L0_xattn_ref(input1, input2, theta_w, theta_b, phi_w, phi_b, g_w, g_b, ln_gamma, ln_beta, out_w, out_b):
        import jax, jax.numpy as jnp
        import numpy as np
        B, DIM1, DIM2, LATENT, T = (16, 128, 128, 64, 256)
        LN_EPS = 1e-05
        theta_x = jnp.einsum('ld,bdt->btl', theta_w, input2) + theta_b
        phi_x = jnp.einsum('ld,bdt->blt', phi_w, input1) + phi_b[:, None]
        scores = jnp.einsum('btl,bls->bts', theta_x, phi_x)
        p = jax.nn.softmax(scores, axis=-1)
        g_x = jnp.einsum('ld,bdt->btl', g_w, input1) + g_b
        t_x = jnp.einsum('bts,bsl->blt', p, g_x)
        mu = jnp.mean(t_x, axis=(1, 2), keepdims=True)
        var = jnp.var(t_x, axis=(1, 2), keepdims=True)
        h = (t_x - mu) * jax.lax.rsqrt(var + LN_EPS) * ln_gamma + ln_beta
        h = jax.nn.relu(h)
        w_t = jnp.einsum('ol,blt->bot', out_w, h) + out_b[None, :, None]
        return w_t + input2

    def _L0_ffn_ref(x, Wg, W1, W3, W2, Ws1, Ws3, Ws2):
        import jax, jax.numpy as jnp
        import numpy as np
        DIM = 256
        INTER = 176
        E = 16
        TOPK = 4
        G = 4
        TOPK_G = 2
        N_SHARED = 2
        SHARED_INTER = N_SHARED * INTER
        ROUTE_SCALE = 1.0

        def _moe_forward(x, Wg, W1, W3, W2, Ws1, Ws3, Ws2):
            B, S, D = x.shape
            xt = x.reshape(-1, D)
            T = xt.shape[0]
            scores = jax.nn.softmax(xt @ Wg.T, axis=-1)
            sg = scores.reshape(T, G, E // G)
            group_scores = sg.max(axis=-1)
            gidx = jax.lax.top_k(group_scores, TOPK_G)[1]
            gmask = jax.nn.one_hot(gidx, G, dtype=jnp.float32).sum(axis=1) > 0
            masked = jnp.where(gmask[:, :, None], sg, -jnp.inf).reshape(T, E)
            topi = jax.lax.top_k(masked, TOPK)[1]
            weights = jnp.take_along_axis(scores, topi, axis=1) * ROUTE_SCALE
            combine = jnp.zeros((T, E), xt.dtype).at[jnp.arange(T)[:, None], topi].add(weights)
            h = jax.nn.silu(jnp.einsum('td,eid->eti', xt, W1)) * jnp.einsum('td,eid->eti', xt, W3)
            expert_out = jnp.einsum('eti,edi->etd', h, W2)
            y = jnp.einsum('etd,te->td', expert_out, combine)
            z = jax.nn.silu(xt @ Ws1.T) * (xt @ Ws3.T) @ Ws2.T
            return (y + z).reshape(B, S, D)
        return _moe_forward(x, Wg, W1, W3, W2, Ws1, Ws3, Ws2)
    x = x + _L0_xattn_ref(_layernorm(x, axis=-1), ctx_2048, L0_xattn_theta_w, L0_xattn_theta_b, L0_xattn_phi_w, L0_xattn_phi_b, L0_xattn_g_w, L0_xattn_g_b, L0_xattn_ln_gamma, L0_xattn_ln_beta, L0_xattn_out_w, L0_xattn_out_b)
    x = x + _L0_ffn_ref(_layernorm(x, axis=-1), L0_ffn_Wg, L0_ffn_W1, L0_ffn_W3, L0_ffn_W2, L0_ffn_Ws1, L0_ffn_Ws3, L0_ffn_Ws2)
    return x

_drawn_inputs = setup_inputs


def setup_inputs(seed=0):
    import zlib

    import numpy as np

    out = dict(_drawn_inputs(seed))
    spreads = {'L0_xattn_theta_b': (0.0, 0.1),
     'L0_xattn_phi_b': (0.0, 2.0),
     'L0_xattn_g_b': (0.0, 0.1),
     'L0_xattn_ln_gamma': (1.0, 0.2),
     'L0_xattn_ln_beta': (0.0, 0.1),
     'L0_xattn_out_b': (0.0, 0.534)}
    factors = {'L0_ffn_Wg': 8.0,
     'L0_ffn_W1': 8.0,
     'L0_ffn_W3': 8.0,
     'L0_ffn_W2': 8.0,
     'L0_ffn_Ws1': 4.418,
     'L0_ffn_Ws3': 4.368,
     'L0_ffn_Ws2': 4.372}
    for name, (base, spread) in spreads.items():
        noise = np.random.default_rng([zlib.crc32(name.encode()), seed]).standard_normal(out[name].shape)
        drawn = base * np.exp(spread * noise) if base else spread * noise
        out[name] = jnp.asarray(drawn.astype(out[name].dtype))
    for name, factor in factors.items():
        out[name] = (out[name] * factor).astype(out[name].dtype)
    return out
```

```python
from contextlib import ExitStack

import numpy as np

import concourse.bass as bass
from concourse import mybir

ALU = mybir.AluOpType
ACT = mybir.ActivationFunctionType
AX = mybir.AxisListType
F32 = mybir.dt.float32
F16 = mybir.dt.float16
I32 = mybir.dt.int32
U32 = mybir.dt.uint32

P = 128
B = 16
T = 256
L = 64
NE = 16
NU = NE + 2
NF = 176
FC = NF // 2
NG = 4
TOPG = 2
TOPK = 4
EPS = 1e-5
WS = 64.0
REGION = B * P + P
NT = (B * P * TOPK + NE * (P - 1)) // P + 1
NT += NT % 2
SLOTS = NE * REGION
UP1 = 2 * NF
W13 = 2 * 2 * UP1
W2 = 2 * 2 * T

COLS = {}
_at = 0
for _n, _w in (("ident", P), ("mean", P), ("lower", NG * NG), ("rank", TOPK * NE), ("carry", 4 * NE),
               ("base", NE), ("tau", NT), ("half", NE), ("gamma", 2 * L), ("beta", 2 * L), ("gb", 2 * L),
               ("thw", L), ("phw", L), ("gw", L), ("wg", 2 * NE), ("outw", P), ("outb", 1), ("thb", 1), ("phb", 1)):
    COLS[_n] = (_at, _at + _w)
    _at += _w
NCOLS = _at


def build(nc, x, ctx_in, params, halves, w13_in, w2_in, out):
    scatter_rows = nc.dram_tensor("slot_rows", (SLOTS, 2 * T), F16, kind="Internal").ap()
    slot_y = nc.dram_tensor("slot_y", (NT * P, T), F32, kind="Internal").ap()

    with ExitStack() as stack:
        def sb(name, shape, dt=F32):
            return stack.enter_context(nc.sbuf_tensor(name, shape, dt))

        def sem(name):
            return stack.enter_context(nc.semaphore(name))

        def span(at, n):
            return slice(at, at + n) if isinstance(at, int) else bass.ds(at, n)

        def wait(eng, s, n):
            if not isinstance(n, int) or n > 0:
                eng.wait_ge(s, n)

        def own_wait(eng):
            eng.nop(nofuse=True)

        par = sb("par", [P, NCOLS])
        hal = sb("hal", [P, 3 * P], F16)
        ident16, tri16, ones16 = hal[:, 0:P], hal[:, P:2 * P], hal[:, 2 * P:3 * P]

        def c(name, rows=P):
            a, b = COLS[name]
            return par[0:rows, a:b]

        x_all = sb("x_all", [P, B * T])
        ctx_all = sb("ctx_all", [P, B * T])
        rows_all = sb("rows_all", [P, B * 2 * T], F16)
        xT_all = sb("xT_all", [P, B * 4 * P], F16)
        w13 = sb("w13", [P, NU * W13], F16)
        w2 = sb("w2", [FC, NU * W2], F16)
        wst13 = sb("wst13", [P, 2, 2 * UP1])
        wst2 = sb("wst2", [FC, 2, 2 * T])
        wg16 = sb("wg16", [P, 2, 2 * NE], F16)
        st1 = sb("st1", [P, B, 6])
        mv1 = sb("mv1", [P, B, 2])
        r1 = sb("r1", [P, B])
        xn = sb("xn", [P, 2, T])
        th = sb("th", [L, 2, T])
        ph = sb("ph", [L, 2, T])
        g_sb = sb("g_sb", [P, 2, 2 * L])
        nmax = sb("nmax", [P, 2, 2])
        psums = sb("psums", [P, 2, 2])
        rsum = sb("rsum", [P, 2, 2])
        p_sb = sb("p_sb", [P, 2, 2 * T])
        pT = sb("pT", [P, 2, 2 * T])
        tx = sb("tx", [P, 2, 2 * L])
        tst = sb("tst", [P, 2, 6])
        tmv = sb("tmv", [P, 2, 2])
        gmv = sb("gmv", [P, 2, 2])
        vneg = sb("vneg", [P, 2])
        vpos = sb("vpos", [P, 2])
        trs = sb("trs", [P, 2])
        hc = sb("hc", [P, 2, 2 * L])
        hpre = sb("hpre", [P, 2, 2 * L])
        hr = sb("hr", [L, 2, T])
        st2 = sb("st2", [P, 2, 6])
        mv2 = sb("mv2", [P, 2, 2])
        v2 = sb("v2", [P, 2])
        r2 = sb("r2", [P, 2])
        xn2 = sb("xn2", [P, 2, T])
        Q = 4
        lg = sb("lg", [P, Q * NE])
        qm = sb("qm", [P, Q])
        qs = sb("qs", [P, Q])
        qr = sb("qr", [P, Q])
        qz = sb("qz", [P, Q * NE])
        qe = sb("qe", [P, Q * NE])
        score = sb("score", [P, Q * NE])
        gmax = sb("gmax", [P, Q * NG])
        gcmp = sb("gcmp", [P, Q * NG * NG])
        geq = sb("geq", [P, Q * NG * NG])
        grank = sb("grank", [P, Q * NG])
        gsel = sb("gsel", [P, Q * NG])
        gsub = sb("gsub", [P, Q * NG])
        masked = sb("masked", [P, Q * NE])
        top8 = sb("top8", [P, Q * 8])
        repl = sb("repl", [P, Q * NE])
        sel = sb("sel", [P, Q * NE])
        sel16 = sb("sel16", [P, Q * NE], F16)
        cum = sb("cum", [P, Q * NE])
        base = sb("base", [P, NE])
        slot = sb("slot", [P, Q * NE])
        onek = sb("onek", [P, Q * TOPK * NE])
        onev = sb("onev", [P, Q * TOPK * NE])
        slot_f = sb("slot_f", [P, B * TOPK])
        slot_c = sb("slot_c", [P, B * TOPK])
        yslot_k = sb("yslot_k", [P, B * TOPK], U32)
        slot_k = sb("slot_k", [P, B * TOPK], U32)
        wt_k = sb("wt_k", [P, B * TOPK])
        zeros16 = sb("zeros16", [P, 2 * T], F16)
        shift = sb("shift", [P, NE])
        cnt = sb("cnt", [P, NE])
        cnt_i = sb("cnt_i", [P, NE], I32)
        nt_a = sb("nt_a", [P, NE])
        nt_i = sb("nt_i", [P, NE], I32)
        nt_s = sb("nt_s", [P, NE], I32)
        nt_f = sb("nt_f", [P, NE])
        ntc = sb("ntc", [P, NE])
        te = sb("te", [1, NT])
        tst0 = sb("tst0", [1, NT])
        trow = sb("trow", [1, NT])
        tval = sb("tval", [1, NT])
        row_i = sb("row_i", [1, NT], I32)
        exp_i = sb("exp_i", [1, NT], I32)
        silu = sb("silu", [P, 2, NF])
        hid = sb("hid", [P, 2, NF])
        hh = sb("hh", [P, 2, 2 * NF], F16)
        hT = sb("hT", [FC, 2, 4 * P], F16)
        m = NT * NE
        ind, indc = ctx_all[0:1, 0:m], ctx_all[0:1, m:2 * m]
        xg = ctx_all[:, 2 * m:2 * m + 2 * T].bitcast(F16).rearrange("p (j c) -> p j c", j=2)
        xT = ctx_all[:, 2 * m + 2 * T:2 * m + 4 * T].bitcast(F16).rearrange("p (j c) -> p j c", j=2)
        y_sb = ctx_all[:, 2 * m + 4 * T:2 * m + 6 * T].rearrange("p (j c) -> p j c", j=2)
        RING = 4
        yg = ctx_all[:, :].rearrange("p (r k t) -> p r k t", r=RING, k=TOPK)

        bank = [stack.enter_context(nc.psum_tensor(f"bank{i}", [P, 512], F32)) for i in range(8)]
        TP, GP, SP_, PT, TS, HO, XB, LB = [b[:, :] for b in bank]
        XB16 = XB.bitcast(F16)[:, 0:4 * P]

        par_in, ctx_in_s, wst_in0, wst_in1 = sem("par_in"), sem("ctx_loaded"), sem("wst_in0"), sem("wst_in1")
        x_in = [sem(f"x_in{i}") for i in range(4)]
        wst_in = [wst_in0, wst_in1]
        names = ("stat_done aggr_done r1_eps r1_done wg_hi wg_lo base_set xn_ready xc_ready tp_mm thph_ready g_mm g_ready s_mm max_ready "
                 "p_ready pt_mm pt_ready rs_ready t_mm tx_ready ts_done ta_done tmv_ready st_mm gmv_done vneg_ready "
                 "v_done trs_ready hc_done hpre_ready ht_mm hr_ready o_mm xr_ready st2_done mv2_ready v2_done "
                 "r2_ready xn2_ready hi_ready lo_ready xt_mm xt_ready l_mm lg_ready wh_ready wl_ready "
                 "route_z route_e route_v sel_ready pre_mm pre_read slot_ready scattered zero_set counts_ready "
                 "table_v yslot_ready table_ready tails_in gathered_all out_written acc_v").split()
        S = {n: sem(n) for n in names}
        gath = [sem(f"gathered{i}") for i in range(RING)]
        acc_done = sem("acc_done")

        FFN = "xt_mm xt_ready up_mm silu_ready h_ready hhi_ready hlo_ready ht_mm hT_ready dn_mm y_ready".split()
        SH = {n: sem(f"sh_{n}") for n in FFN}
        EX = {n: sem(f"ex_{n}") for n in FFN}

        xg_in = [sem("xg_in0"), sem("xg_in1")]
        y_out = [sem("y_out0"), sem("y_out1")]

        FIRST, LAST = 4, 16
        STEPS = B + 2

        def pipeline(eng, step):
            for s in range(FIRST):
                step(s, s)
            with eng.Fori(FIRST, LAST - 3, 4) as i:
                for v in range(4):
                    step(i + v, v)
            for s in range(LAST, STEPS):
                step(s, s % 4)

        def does(s, lag):
            return not isinstance(s, int) or 0 <= s - lag < B

        def routes(s, v):
            return v == 1 and (not isinstance(s, int) or s >= 5)

        def expert_pipeline(eng, step):
            for s in range(4):
                step(s, s % 2)
            with eng.Fori(4, NT - 1, 2) as i:
                for v in range(2):
                    step(i + v, v)
            for s in range(NT, NT + 3):
                step(s, s % 2)

        def has(s, lag):
            return not isinstance(s, int) or 0 <= s - lag < NT

        def shared_pipeline(eng, step):
            for u in range(2):
                step(0, u)
            with eng.Fori(1, B) as b:
                for u in range(2):
                    step(b, u)
            for u in range(2):
                step(B, u)

        def shared(n, lag):
            return not isinstance(n, int) or 0 <= n - lag < 2 * B

        U, H, Y = [TP, GP], [SP_, PT], [TS, HO]
        X16 = [b.bitcast(F16)[:, 0:4 * P] for b in (XB, LB)]
        H16 = [h.bitcast(F16)[0:FC, 0:4 * P] for h in H]

        block = stack.enter_context(nc.Block())

        @block.sync
        def _(sp):
            sp.dma_start(par[:, :], params).then_inc(par_in, 16)
            sp.dma_start(hal[:, :], halves).then_inc(par_in, 16)
            xv = x.rearrange("b p t -> p b t")
            cv = ctx_in.rearrange("b p t -> p b t")
            x3 = x_all[:, :].rearrange("p (b t) -> p b t", t=T)
            c3 = ctx_all[:, :].rearrange("p (b t) -> p b t", t=T)
            for n in range(4):
                sp.dma_start(x3[:, 4 * n:4 * n + 4, :], xv[:, 4 * n:4 * n + 4, :]).then_inc(x_in[n], 16)
            sp.dma_start(c3, cv).then_inc(ctx_in_s, 16)

            def load_weights(e, j):
                wait(sp, S["wl_ready"], e - 1)
                sp.dma_start(wst13[:, j, :], w13_in[span(e, 1), :, :].rearrange("a p f -> (a p) f")).then_inc(wst_in[j], 16)
                sp.dma_start(wst2[:, j, :], w2_in[span(e, 1), :, :].rearrange("a p f -> (a p) f")).then_inc(wst_in[j], 16)

            for e in range(2):
                load_weights(e, e)
            with sp.Fori(2, NU - 1, 2) as e:
                load_weights(e, 0)
                load_weights(e + 1, 1)

            sp.wait_ge(S["zero_set"], 1)
            sp.wait_ge(S["counts_ready"], 1)
            with sp.Fori(0, NE) as e:
                n = sp.value_load(cnt_i[0:1, span(e, 1)], min_val=0, max_val=B * P)
                sp.dma_start(scatter_rows[bass.ds(e * REGION + n, P), :], zeros16[:, :]).then_inc(S["tails_in"], 16)

            sp.wait_ge(S["tails_in"], 16 * NE)
            sp.wait_ge(S["scattered"], 16 * B * TOPK)
            sp.wait_ge(S["table_ready"], 1)

            def load_tile(t, j):
                wait(sp, EX["xt_mm"], t - 1)
                r = sp.value_load(row_i[0:1, span(t, 1)], min_val=0, max_val=SLOTS - P)
                sp.dma_start(xg[:, j, :], scatter_rows[bass.ds(r, P), :]).then_inc(xg_in[j], 16)

            for t in range(2):
                load_tile(t, t)
            with sp.Fori(2, NT - 1, 2) as t:
                load_tile(t, 0)
                load_tile(t + 1, 1)

            ov = out.rearrange("b p t -> (b p) t")
            with sp.Fori(0, B) as b:
                sp.wait_ge(acc_done, b + 1)
                sp.dma_start(ov[bass.ds(b * P, P), :], x_all[:, span(b * T, T)]).then_inc(S["out_written"], 16)
            sp.wait_ge(S["out_written"], 16 * B)

        @block.scalar
        def _(act):
            A = nc.scalar.activation
            act.wait_ge(par_in, 32)

            def weights_high(s, v):
                j = v % 2
                act.wait_ge(wst_in[j], 16 * s + 32 - 16 * j)
                A(w13[:, span(s * W13, 2 * UP1)], wst13[:, j, :], ACT.Copy, scale=WS)
                A(w2[:, span(s * W2, 2 * T)], wst2[:, j, :], ACT.Copy, scale=WS).then_inc(S["wh_ready"], 1)

            def theta_phi(b, j):
                act.wait_ge(S["tp_mm"], b + 1)
                wait(act, S["s_mm"], b - 1)
                A(th[:, j, :], TP[0:L, 0:T], ACT.Identity, bias=c("thb", L))
                A(ph[:, j, :], TP[0:L, T:2 * T], ACT.Identity, bias=c("phb", L)).then_inc(S["thph_ready"], 1)

            def exps(b, j):
                act.wait_ge(S["max_ready"], b + 1)
                wait(act, S["pt_mm"], b - 1)
                wait(act, S["rs_ready"], b - 1)
                for h in range(2):
                    i = A(p_sb[:, j, h * T:(h + 1) * T], SP_[:, h * T:(h + 1) * T], ACT.Exp,
                          bias=nmax[:, j, h:h + 1], accum_out=psums[:, j, h:h + 1])
                i.then_inc(S["p_ready"], 1)

            def copy_pT(b, j):
                act.wait_ge(S["pt_mm"], b + 1)
                wait(act, S["t_mm"], b - 1)
                A(pT[:, j, :], PT, ACT.Copy).then_inc(S["pt_ready"], 1)

            def relu(b, j):
                act.wait_ge(S["ht_mm"], b + 1)
                wait(act, S["o_mm"], b - 1)
                A(hr[:, j, :], HO[0:L, 0:T], ACT.Relu).then_inc(S["hr_ready"], 1)

            def high(b, j):
                act.wait_ge(S["xn2_ready"], b + 1)
                A(rows_all[:, span(b * 2 * T, T)], xn2[:, j, :], ACT.Copy).then_inc(S["hi_ready"], 1)

            def step(s, v):
                if does(s, 0):
                    theta_phi(s, v % 2)
                if does(s, 2):
                    high(s - 2, v % 2)
                if does(s, 0):
                    exps(s, v % 2)
                if does(s, 1):
                    relu(s - 1, (v + 1) % 2)
                if does(s, 0):
                    copy_pT(s, v % 2)
                weights_high(s, v)
                if routes(s, v):
                    act.wait_ge(S["route_z"], s - 1)
                    A(qe[:, :], qz[:, :], ACT.Exp).then_inc(S["route_e"], 4)

            pipeline(act, step)

            def gate(G, n, j):
                act.wait_ge(G["up_mm"], n + 1)
                wait(act, G["h_ready"], n - 1)
                A(silu[:, j, :], U[j][:, 0:NF], ACT.Silu, scale=1 / WS).then_inc(G["silu_ready"], 1)

            def hidden_high(G, n, j):
                act.wait_ge(G["h_ready"], n + 1)
                wait(act, G["ht_mm"], n - 1)
                A(hh[:, j, 0:NF], hid[:, j, :], ACT.Copy).then_inc(G["hhi_ready"], 1)

            def sstep(b, u):
                n = 2 * b + u
                if shared(n, 0):
                    gate(SH, n, u)
                    hidden_high(SH, n, u)

            shared_pipeline(act, sstep)

            def estep(s, v):
                k = (v + 1) % 2
                if has(s, 1):
                    gate(EX, s - 1, k)
                if has(s, 3):
                    t = s - 3
                    act.wait_ge(EX["dn_mm"], t + 1)
                    wait(act, y_out[k], 8 * (t - k))
                    A(y_sb[:, k, :], Y[k][:, 0:T], ACT.Copy, scale=1 / WS).then_inc(EX["y_ready"], 1)
                if has(s, 1):
                    hidden_high(EX, s - 1, k)

            expert_pipeline(act, estep)

        @block.tensor
        def _(pe):
            mm, tr = nc.tensor.matmul, nc.tensor.transpose
            ident = c("ident")
            pe.wait_ge(par_in, 32)
            pe.wait_ge(ctx_in_s, 16)

            def project(b, j):
                wait(pe, S["thph_ready"], b)
                mm(TP[0:L, 0:T], c("thw"), ctx_all[:, span(b * T, T)], start=True, stop=True)
                pe.wait_ge(S["xn_ready"], b + 1)
                mm(TP[0:L, T:2 * T], c("phw"), xn[:, j, :], start=True, stop=True).then_inc(S["tp_mm"], 1)
                wait(pe, S["g_ready"], b)
                for h in range(2):
                    i = mm(GP[:, h * L:(h + 1) * L], xn[:, j, h * P:(h + 1) * P], c("gw"), start=True, stop=True)
                i.then_inc(S["g_mm"], 1)

            def scores(b, j):
                pe.wait_ge(S["thph_ready"], b + 1)
                wait(pe, S["p_ready"], b)
                for h in range(2):
                    i = mm(SP_[:, h * T:(h + 1) * T], th[:, j, h * P:(h + 1) * P], ph[:, j, :], start=True, stop=True)
                i.then_inc(S["s_mm"], 1)

            def transpose_p(b, j):
                pe.wait_ge(S["p_ready"], b + 1)
                wait(pe, S["pt_ready"], b)
                for h in range(2):
                    for k in range(2):
                        i = tr(PT[:, k * T + h * P:k * T + h * P + P], p_sb[:, j, h * T + k * P:h * T + k * P + P], ident)
                i.then_inc(S["pt_mm"], 1)

            def attend(b, j):
                pe.wait_ge(S["pt_ready"], b + 1)
                pe.wait_ge(S["g_ready"], b + 1)
                wait(pe, S["gmv_done"], b)
                for h in range(2):
                    for k in range(2):
                        i = mm(TS[:, h * L:(h + 1) * L], pT[:, j, k * T + h * P:k * T + h * P + P],
                               g_sb[:, j, k * L:(k + 1) * L], start=k == 0, stop=k == 1)
                i.then_inc(S["t_mm"], 1)

            def mean_all(b, j):
                pe.wait_ge(S["tmv_ready"], b + 1)
                mm(TS[:, 2 * L:2 * L + 2], c("mean"), tmv[:, j, :], start=True, stop=True).then_inc(S["st_mm"], 1)

            def transpose_h(b, j):
                pe.wait_ge(S["hpre_ready"], b + 1)
                wait(pe, S["xr_ready"], b)
                own_wait(pe)
                for h in range(2):
                    i = tr(HO[0:L, h * P:(h + 1) * P], hpre[:, j, h * L:(h + 1) * L], ident)
                i.then_inc(S["ht_mm"], 1)

            def project_out(b, j):
                pe.wait_ge(S["hr_ready"], b + 1)
                mm(HO[:, T:2 * T], c("outw", L), hr[:, j, :], start=True, stop=True).then_inc(S["o_mm"], 1)

            def transpose_rows(b):
                pe.wait_ge(S["lo_ready"], b + 1)
                wait(pe, S["xt_ready"], b)
                for k in range(4):
                    i = tr(XB16[:, k * P:(k + 1) * P], rows_all[:, span(b * 2 * T + k * P, P)], ident16)
                i.then_inc(S["xt_mm"], 1)

            def router(b, u):
                pe.wait_ge(S["xt_ready"], b + 1)
                wait(pe, S["lg_ready"], b)
                if u == 0 and (not isinstance(b, int) or b > 0):
                    pe.wait_ge(S["pre_read"], b)
                for k in range(4):
                    for w in range(2):
                        i = mm(LB[:, u * NE:(u + 1) * NE], xT_all[:, span((b * 4 + k) * P, P)],
                               wg16[:, k % 2, w * NE:(w + 1) * NE], start=k == 0 and w == 0, stop=k == 3 and w == 1)
                i.then_inc(S["l_mm"], 1)

            def count(s):
                pe.wait_ge(S["sel_ready"], s - 1)
                pe.wait_ge(S["lg_ready"], s - 1)
                for u in range(4):
                    for v in range(u + 1):
                        mm(LB[:, 64 + u * NE:64 + (u + 1) * NE], tri16 if v == u else ones16,
                           sel16[:, v * NE:(v + 1) * NE], start=v == 0, stop=v == u)
                for v in range(4):
                    i = mm(LB[:, 128:128 + NE], ones16, sel16[:, v * NE:(v + 1) * NE], start=v == 0, stop=v == 3)
                i.then_inc(S["pre_mm"], 4)

            def step(s, v):
                j, k = v % 2, (v + 1) % 2
                if does(s, 0):
                    project(s, j)
                if does(s, 1):
                    attend(s - 1, k)
                if does(s, 2):
                    transpose_rows(s - 2)
                if does(s, 0):
                    scores(s, j)
                if does(s, 1):
                    mean_all(s - 1, k)
                if does(s, 2):
                    if not isinstance(s, int) or s == 2:
                        pe.wait_ge(S["wg_lo"], 1)
                    router(s - 2, (v + 2) % 4)
                if does(s, 1):
                    transpose_h(s - 1, k)
                if does(s, 0):
                    transpose_p(s, j)
                if does(s, 1):
                    project_out(s - 1, k)
                if routes(s, v):
                    count(s)

            pipeline(pe, step)

            def up(G, n, j, xt, wcol):
                first = True
                for part, wpart in ((0, 0), (0, 1), (1, 0)):
                    for k in range(2):
                        i = mm(U[j][:, 0:UP1], xt(2 * part + k), w13[:, span(wcol + (2 * wpart + k) * UP1, UP1)],
                               start=first, stop=part == 1 and k == 1)
                        first = False
                i.then_inc(G["up_mm"], 1)

            def transpose_hidden(G, n, j):
                pe.wait_ge(G["hlo_ready"], n + 1)
                wait(pe, G["hT_ready"], n - 1)
                for k in range(4):
                    i = tr(H16[j][:, k * P:(k + 1) * P], hh[:, j, k * FC:(k + 1) * FC], ident16)
                i.then_inc(G["ht_mm"], 1)

            def down(G, n, j, y, wcol, start, stop):
                pe.wait_ge(G["hT_ready"], n + 1)
                first = start
                for part, wpart in ((0, 0), (0, 1), (1, 0)):
                    for k in range(2):
                        i = mm(y[:, 0:T], hT[:, j, (2 * part + k) * P:(2 * part + k + 1) * P],
                               w2[:, span(wcol + (2 * wpart + k) * T, T)], start=first, stop=stop and part == 1 and k == 1)
                        first = False
                i.then_inc(G["dn_mm"], 1)

            pe.wait_ge(S["wl_ready"], NU)
            for n in ("thph_ready", "g_ready", "p_ready", "pt_ready", "gmv_done", "xr_ready", "xt_ready", "pre_read"):
                pe.wait_ge(S[n], B)

            def sstep(b, u):
                n = 2 * b + u
                if shared(n, 0):
                    wait(pe, SH["h_ready"], n - 1)
                    up(SH, n, u, lambda k: xT_all[:, span((b * 4 + k) * P, P)], (NE + u) * W13)
                if shared(n, 1):
                    transpose_hidden(SH, n - 1, 1 - u)
                if shared(n, 2):
                    if u == 0:
                        wait(pe, SH["y_ready"], b - 1)
                    down(SH, n - 2, u, Y[0], (NE + u) * W2, start=u == 0, stop=u == 1)

            shared_pipeline(pe, sstep)

            pe.wait_ge(S["table_ready"], 1)
            pe.wait_ge(SH["y_ready"], B)

            def estep(s, v):
                k = (v + 1) % 2
                if has(s, 0):
                    pe.wait_ge(xg_in[v], 8 * (s - v) + 16)
                    wait(pe, EX["xt_ready"], s - 1)
                    for q in range(4):
                        i = tr(X16[v][:, q * P:(q + 1) * P], xg[:, v, q * P:(q + 1) * P], ident16)
                    i.then_inc(EX["xt_mm"], 1)
                if has(s, 1):
                    e = pe.value_load(exp_i[0:1, span(s - 1, 1)], min_val=0, max_val=NE - 1)
                    pe.wait_ge(EX["xt_ready"], s)
                    wait(pe, EX["h_ready"], s - 2)
                    up(EX, s - 1, k, lambda q: xT[:, k, q * P:(q + 1) * P], e * W13)
                if has(s, 2):
                    transpose_hidden(EX, s - 2, v)
                if has(s, 3):
                    e = pe.value_load(exp_i[0:1, span(s - 3, 1)], min_val=0, max_val=NE - 1)
                    wait(pe, EX["y_ready"], s - 4)
                    down(EX, s - 3, k, Y[k], e * W2, start=True, stop=True)

            expert_pipeline(pe, estep)

        @block.vector
        def _(dve):
            V = nc.vector
            rows3 = lambda a, n: a[:, :].rearrange("p (q e) -> p q e", e=n)

            for b in range(B):
                if b % 4 == 0:
                    dve.wait_ge(x_in[b // 4], 16)
                V.bn_stats(st1[:, b, :], x_all[:, b * T:(b + 1) * T]).then_inc(S["stat_done"], 1)
            for b in range(B):
                dve.wait_ge(S["stat_done"], b + 1)
                V.bn_aggr(mv1[:, b, :], st1[:, b, :]).then_inc(S["aggr_done"], 1)
            dve.wait_ge(par_in, 32)
            V.memset(zeros16[:, :], 0.0).then_inc(S["zero_set"], 1)
            V.tensor_scalar(wg16[:, :, 0:NE], c("wg").rearrange("p (k e) -> p k e", e=NE), WS, None, ALU.mult).then_inc(S["wg_hi"], 1)
            V.tensor_copy(base[:, :], c("base")).then_inc(S["base_set"], 1)
            dve.wait_ge(S["wg_hi"], 1)
            V.scalar_tensor_tensor(wg16[:, :, NE:2 * NE], c("wg").rearrange("p (k e) -> p k e", e=NE), WS,
                                   wg16[:, :, 0:NE], ALU.mult, ALU.subtract).then_inc(S["wg_lo"], 1)
            dve.wait_ge(S["r1_done"], 1)

            def normalise(b, j):
                wait(dve, S["g_mm"], b - 1)
                V.tensor_scalar(xn[:, j, :], x_all[:, span(b * T, T)], mv1[:, span(b, 1), 0:1].rearrange("p a c -> p (a c)"),
                                r1[:, span(b, 1)], ALU.subtract, ALU.mult).then_inc(S["xn_ready"], 1)

            def values(b, j):
                dve.wait_ge(S["g_mm"], b + 1)
                wait(dve, S["t_mm"], b - 1)
                V.tensor_tensor(g_sb[:, j, :], GP[:, 0:2 * L], c("gb"), ALU.add).then_inc(S["g_ready"], 1)

            def row_max(b, j):
                dve.wait_ge(S["s_mm"], b + 1)
                wait(dve, S["p_ready"], b - 1)
                V.tensor_reduce(nmax[:, j, :], SP_.rearrange("p (h t) -> p h t", h=2), AX.X, ALU.max, negate=True).then_inc(S["max_ready"], 1)

            def latent(b, j):
                dve.wait_ge(S["p_ready"], b + 1)
                V.reciprocal(rsum[:, j, :], psums[:, j, :]).then_inc(S["rs_ready"], 1)
                dve.wait_ge(S["rs_ready"], b + 1)
                dve.wait_ge(S["t_mm"], b + 1)
                V.tensor_tensor(tx[:, j, :].rearrange("p (h l) -> p h l", h=2), TS[:, 0:2 * L].rearrange("p (h l) -> p h l", h=2),
                                rsum[:, j, :].unsqueeze(2).broadcast_to([P, 2, L]), ALU.mult).then_inc(S["tx_ready"], 1)
                dve.wait_ge(S["tx_ready"], b + 1)
                own_wait(dve)
                V.bn_stats(tst[:, j, :], tx[:, j, :]).then_inc(S["ts_done"], 1)
                dve.wait_ge(S["ts_done"], b + 1)
                own_wait(dve)
                V.bn_aggr(tmv[:, j, :], tst[:, j, :]).then_inc(S["ta_done"], 1)
                dve.wait_ge(S["ta_done"], b + 1)
                V.scalar_tensor_tensor(tmv[:, j, 1:2], tmv[:, j, 0:1], tmv[:, j, 0:1], tmv[:, j, 1:2], ALU.mult, ALU.add).then_inc(S["tmv_ready"], 1)

            def latent_norm(b, j):
                dve.wait_ge(S["st_mm"], b + 1)
                V.tensor_copy(gmv[:, j, :], TS[:, 2 * L:2 * L + 2]).then_inc(S["gmv_done"], 1)
                dve.wait_ge(S["gmv_done"], b + 1)
                wait(dve, S["trs_ready"], b - 1)
                V.scalar_tensor_tensor(vneg[:, j:j + 1], gmv[:, j, 0:1], gmv[:, j, 0:1], gmv[:, j, 1:2],
                                       ALU.mult, ALU.subtract).then_inc(S["vneg_ready"], 1)
                V.scalar_tensor_tensor(hc[:, j, :], tx[:, j, :], gmv[:, j, 0:1], c("gamma"), ALU.subtract, ALU.mult).then_inc(S["hc_done"], 1)

            def latent_out(b, j):
                dve.wait_ge(S["hc_done"], b + 1)
                dve.wait_ge(S["trs_ready"], b + 1)
                wait(dve, S["ht_mm"], b - 1)
                V.scalar_tensor_tensor(hpre[:, j, :], hc[:, j, :], trs[:, j:j + 1], c("beta"), ALU.mult, ALU.add).then_inc(S["hpre_ready"], 1)

            def residual(b, j):
                dve.wait_ge(S["o_mm"], b + 1)
                dve.wait_ge(S["xc_ready"], b + 1)
                xs = x_all[:, span(b * T, T)]
                V.scalar_tensor_tensor(xs, HO[:, T:2 * T], c("outb"), xs, ALU.add, ALU.add).then_inc(S["xr_ready"], 1)

            def stats2(b, j):
                dve.wait_ge(S["xr_ready"], b + 1)
                own_wait(dve)
                V.bn_stats(st2[:, j, :], x_all[:, span(b * T, T)]).then_inc(S["st2_done"], 1)
                dve.wait_ge(S["st2_done"], b + 1)
                wait(dve, S["r2_ready"], b - 1)
                own_wait(dve)
                V.bn_aggr(mv2[:, j, :], st2[:, j, :]).then_inc(S["mv2_ready"], 1)

            def normalise2(b, j):
                dve.wait_ge(S["r2_ready"], b + 1)
                wait(dve, S["hi_ready"], b - 1)
                V.tensor_scalar(xn2[:, j, :], x_all[:, span(b * T, T)], mv2[:, j, 0:1], r2[:, j:j + 1],
                                ALU.subtract, ALU.mult).then_inc(S["xn2_ready"], 1)

            def low(b, j):
                dve.wait_ge(S["hi_ready"], b + 1)
                V.tensor_tensor(rows_all[:, span(b * 2 * T + T, T)], xn2[:, j, :], rows_all[:, span(b * 2 * T, T)],
                                ALU.subtract).then_inc(S["lo_ready"], 1)

            def copy_xT(b):
                dve.wait_ge(S["xt_mm"], b + 1)
                V.tensor_copy(xT_all[:, span(b * 4 * P, 4 * P)], XB16).then_inc(S["xt_ready"], 1)

            def logits(b, u):
                dve.wait_ge(S["l_mm"], b + 1)
                V.tensor_scalar(lg[:, u * NE:(u + 1) * NE], LB[:, u * NE:(u + 1) * NE], 1 / WS, None, ALU.mult).then_inc(S["lg_ready"], 1)

            def weights_low(s, v):
                j = v % 2
                dve.wait_ge(S["wh_ready"], s + 1)
                V.scalar_tensor_tensor(w13[:, span(s * W13 + 2 * UP1, 2 * UP1)], wst13[:, j, :], WS,
                                       w13[:, span(s * W13, 2 * UP1)], ALU.mult, ALU.subtract)
                V.scalar_tensor_tensor(w2[:, span(s * W2 + 2 * T, 2 * T)], wst2[:, j, :], WS,
                                       w2[:, span(s * W2, 2 * T)], ALU.mult, ALU.subtract).then_inc(S["wl_ready"], 1)

            RV = 28

            def route(s):
                r0 = (s - 5) * (RV // 4)
                def after(n):
                    dve.wait_ge(S["route_v"], r0 + n)
                def bc(a, n):
                    return a.unsqueeze(2).broadcast_to([P, a.shape[1], n])
                lg3, z3, e3, sc3, m3 = (rows3(a, NE) for a in (lg, qz, qe, score, masked))
                dve.wait_ge(S["lg_ready"], s - 1)
                V.tensor_reduce(qm[:, :], lg3, AX.X, ALU.max).then_inc(S["route_v"], 1)
                after(1)
                V.tensor_tensor(z3, lg3, bc(qm[:, :], NE), ALU.subtract).then_inc(S["route_z"], 4)
                dve.wait_ge(S["route_e"], s - 1)
                V.tensor_reduce(qs[:, :], e3, AX.X, ALU.add).then_inc(S["route_v"], 1)
                after(2)
                V.reciprocal(qr[:, :], qs[:, :]).then_inc(S["route_v"], 1)
                after(3)
                V.tensor_tensor(sc3, e3, bc(qr[:, :], NE), ALU.mult).then_inc(S["route_v"], 1)
                after(4)
                V.tensor_reduce(gmax[:, :], rows3(score, NG), AX.X, ALU.max).then_inc(S["route_v"], 1)
                after(5)
                gm = gmax[:, :].rearrange("p (q g) -> p q g", g=NG)
                other = gm.unsqueeze(2).broadcast_to([P, Q, NG, NG])
                own = gm.unsqueeze(3).broadcast_to([P, Q, NG, NG])
                c4 = gcmp[:, :].rearrange("p (q g h) -> p q g h", g=NG, h=NG)
                e4 = geq[:, :].rearrange("p (q g h) -> p q g h", g=NG, h=NG)
                V.tensor_tensor(c4, other, own, ALU.is_gt)
                V.tensor_tensor(e4, other, own, ALU.is_equal).then_inc(S["route_v"], 1)
                after(6)
                e3q = geq[:, :].rearrange("p (q g) -> p q g", q=Q)
                V.tensor_tensor(e3q, e3q, c("lower").unsqueeze(1).broadcast_to([P, Q, NG * NG]), ALU.mult).then_inc(S["route_v"], 1)
                after(7)
                V.tensor_tensor(gcmp[:, :], gcmp[:, :], geq[:, :], ALU.add).then_inc(S["route_v"], 1)
                after(8)
                V.tensor_reduce(grank[:, :], gcmp[:, :].rearrange("p (g h) -> p g h", h=NG), AX.X, ALU.add).then_inc(S["route_v"], 1)
                after(9)
                V.tensor_scalar(gsel[:, :], grank[:, :], float(TOPG), None, ALU.is_lt)
                V.tensor_scalar(gsub[:, :], grank[:, :], float(TOPG), -1.0, ALU.is_lt, ALU.add).then_inc(S["route_v"], 1)
                after(10)
                mg, sg = rows3(masked, NG), rows3(score, NG)
                V.tensor_tensor(mg, sg, bc(gsel[:, :], NG), ALU.mult).then_inc(S["route_v"], 1)
                after(11)
                V.tensor_tensor(mg, mg, bc(gsub[:, :], NG), ALU.add).then_inc(S["route_v"], 1)
                after(12)
                own_wait(dve)
                for q in range(Q):
                    i = V.max(top8[:, 8 * q:8 * q + 8], masked[:, q * NE:(q + 1) * NE])
                i.then_inc(S["route_v"], 1)
                after(13)
                V.memset(rows3(top8, 8)[:, :, TOPK:8], -1.0).then_inc(S["route_v"], 1)
                after(14)
                own_wait(dve)
                for q in range(Q):
                    i = V.match_replace(repl[:, q * NE:(q + 1) * NE], top8[:, 8 * q:8 * q + 8], masked[:, q * NE:(q + 1) * NE], -2.0)
                i.then_inc(S["route_v"], 1)
                after(15)
                V.tensor_tensor(sel[:, :], masked[:, :], repl[:, :], ALU.subtract).then_inc(S["route_v"], 1)
                after(16)
                V.tensor_scalar(sel16[:, :], sel[:, :], 2.0, None, ALU.is_ge).then_inc(S["sel_ready"], 4)
                V.tensor_scalar(sel[:, :], sel[:, :], 2.0, None, ALU.is_ge).then_inc(S["route_v"], 1)
                after(17)
                V.tensor_tensor_scan(cum[:, :], c("carry"), sel[:, :], 0.0, ALU.mult, ALU.add).then_inc(S["route_v"], 1)
                after(18)
                V.tensor_tensor(cum[:, :], cum[:, :], sel[:, :], ALU.mult).then_inc(S["route_v"], 1)
                after(19)
                k4 = onek[:, :].rearrange("p (q k e) -> p q k e", q=Q, k=TOPK)
                v4 = onev[:, :].rearrange("p (q k e) -> p q k e", q=Q, k=TOPK)
                by_k = lambda a: rows3(a, NE).unsqueeze(2).broadcast_to([P, Q, TOPK, NE])
                V.tensor_tensor(k4, by_k(cum), c("rank").rearrange("p (k e) -> p k e", k=TOPK).unsqueeze(1).broadcast_to([P, Q, TOPK, NE]),
                                ALU.is_equal).then_inc(S["route_v"], 1)
                after(20)
                V.tensor_tensor(v4, k4, by_k(score), ALU.mult).then_inc(S["route_v"], 1)
                after(21)
                col = (s - 5) * TOPK
                V.tensor_reduce(wt_k[:, span(col, Q * TOPK)], onev[:, :].rearrange("p (q e) -> p q e", e=NE), AX.X, ALU.add).then_inc(S["route_v"], 1)
                dve.wait_ge(S["pre_mm"], s - 1)
                V.tensor_tensor(rows3(slot, NE), LB[:, 64:64 + Q * NE].rearrange("p (q e) -> p q e", e=NE),
                                base[:, :].unsqueeze(1).broadcast_to([P, Q, NE]), ALU.add).then_inc(S["route_v"], 1)
                after(23)
                V.tensor_tensor(base[:, :], base[:, :], LB[:, 128:128 + NE], ALU.add).then_inc(S["pre_read"], 4)
                V.tensor_tensor(v4, k4, by_k(slot), ALU.mult).then_inc(S["route_v"], 1)
                after(24)
                V.tensor_reduce(slot_f[:, span(col, Q * TOPK)], onev[:, :].rearrange("p (q e) -> p q e", e=NE), AX.X, ALU.add).then_inc(S["route_v"], 4)
                after(RV)
                V.tensor_copy(slot_k[:, span(col, Q * TOPK)], slot_f[:, span(col, Q * TOPK)]).then_inc(S["slot_ready"], 4)

            def step(s, v):
                j, k = v % 2, (v + 1) % 2
                if does(s, 0):
                    normalise(s, j)
                if does(s, 2):
                    normalise2(s - 2, j)
                if does(s, 1):
                    latent(s - 1, k)
                if does(s, 0):
                    values(s, j)
                if does(s, 2):
                    low(s - 2, j)
                if does(s, 0):
                    row_max(s, j)
                if does(s, 1):
                    latent_norm(s - 1, k)
                if does(s, 2):
                    copy_xT(s - 2)
                if does(s, 1):
                    latent_out(s - 1, k)
                weights_low(s, v)
                if does(s, 2):
                    logits(s - 2, (v + 2) % 4)
                if does(s, 1):
                    residual(s - 1, k)
                    stats2(s - 1, k)
                if routes(s, v):
                    route(s)

            pipeline(dve, step)

            tv = [0]
            def link(i):
                tv[0] += 1
                i.then_inc(S["table_v"], 1)
                dve.wait_ge(S["table_v"], tv[0])
            dve.wait_ge(S["pre_read"], B)
            link(V.tensor_tensor(cnt[:, :], base[:, :], c("base"), ALU.subtract))
            V.tensor_copy(cnt_i[:, :], cnt[:, :]).then_inc(S["counts_ready"], 1)
            link(V.tensor_scalar(nt_a[:, :], cnt[:, :], float(P - 1), None, ALU.add))
            link(V.tensor_copy(nt_i[:, :], nt_a[:, :]))
            link(V.tensor_scalar(nt_s[:, :], nt_i[:, :], P.bit_length() - 1, None, ALU.logical_shift_right))
            link(V.tensor_copy(nt_f[:, :], nt_s[:, :]))
            link(V.memset(nt_a[:, :], 1.0))
            link(V.tensor_tensor_scan(ntc[:, :], nt_a[:, :], nt_f[:, :], 0.0, ALU.mult, ALU.add))
            i3 = ind.rearrange("p (t e) -> p t e", e=NE)
            c3 = indc.rearrange("p (t e) -> p t e", e=NE)
            ends = ntc[0:1, :].unsqueeze(1).broadcast_to([1, NT, NE])
            link(V.tensor_tensor(i3, ends, c("tau", 1).unsqueeze(2).broadcast_to([1, NT, NE]), ALU.is_le))
            link(V.tensor_reduce(te[:, :], i3, AX.X, ALU.add))
            link(V.tensor_tensor(c3, i3, ends, ALU.mult))
            link(V.tensor_reduce(tst0[:, :], c3, AX.X, ALU.max))
            link(V.tensor_tensor(trow[:, :], c("tau", 1), tst0[:, :], ALU.subtract))
            link(V.tensor_scalar(trow[:, :], trow[:, :], float(P), None, ALU.mult))
            link(V.scalar_tensor_tensor(trow[:, :], te[:, :], float(REGION), trow[:, :], ALU.mult, ALU.add))
            link(V.tensor_scalar(tval[:, :], te[:, :], float(NE), None, ALU.is_lt))
            link(V.tensor_tensor(trow[:, :], trow[:, :], tval[:, :], ALU.mult))
            link(V.tensor_tensor(te[:, :], te[:, :], tval[:, :], ALU.mult))
            link(V.tensor_copy(row_i[:, :], trow[:, :]))
            V.tensor_copy(exp_i[:, :], te[:, :]).then_inc(S["table_ready"], 1)
            link(V.memset(shift[:, :], 0.0))
            link(V.tensor_scalar(shift[:, 1:NE], nt_f[:, 0:NE - 1], float(P), float(-REGION), ALU.mult, ALU.add))
            s3 = ctx_all[:, 0:B * TOPK * NE].rearrange("p (s e) -> p s e", e=NE)
            link(V.tensor_tensor(s3, slot_f[:, :].unsqueeze(2).broadcast_to([P, B * TOPK, NE]),
                                 c("base").unsqueeze(1).broadcast_to([P, B * TOPK, NE]), ALU.is_ge))
            link(V.tensor_tensor(s3, s3, shift[:, :].unsqueeze(1).broadcast_to([P, B * TOPK, NE]), ALU.mult))
            link(V.tensor_reduce(slot_c[:, :], s3, AX.X, ALU.add))
            link(V.tensor_tensor(slot_c[:, :], slot_c[:, :], slot_f[:, :], ALU.add))
            V.tensor_copy(yslot_k[:, :], slot_c[:, :]).then_inc(S["yslot_ready"], 1)

            def hidden(G, n, j):
                dve.wait_ge(G["silu_ready"], n + 1)
                wait(dve, G["hlo_ready"], n - 1)
                V.scalar_tensor_tensor(hid[:, j, :], U[j][:, NF:UP1], 1 / WS, silu[:, j, :], ALU.mult, ALU.mult).then_inc(G["h_ready"], 1)

            def hidden_low(G, n, j):
                dve.wait_ge(G["hhi_ready"], n + 1)
                V.tensor_tensor(hh[:, j, NF:2 * NF], hid[:, j, :], hh[:, j, 0:NF], ALU.subtract).then_inc(G["hlo_ready"], 1)

            def copy_hT(G, n, j):
                dve.wait_ge(G["ht_mm"], n + 1)
                wait(dve, G["dn_mm"], n - 1)
                V.tensor_copy(hT[:, j, :], H16[j]).then_inc(G["hT_ready"], 1)

            def sstep(b, u):
                n = 2 * b + u
                if shared(n, 0):
                    hidden(SH, n, u)
                if shared(n, 1):
                    copy_hT(SH, n - 1, 1 - u)
                if shared(n, 0):
                    hidden_low(SH, n, u)
                if u == 1 and shared(n, 2):
                    dve.wait_ge(SH["dn_mm"], n - 1)
                    xs = x_all[:, span((b - 1) * T, T)]
                    V.scalar_tensor_tensor(xs, Y[0][:, 0:T], 1 / WS, xs, ALU.mult, ALU.add).then_inc(SH["y_ready"], 1)

            shared_pipeline(dve, sstep)

            def estep(s, v):
                k = (v + 1) % 2
                if has(s, 0):
                    dve.wait_ge(EX["xt_mm"], s + 1)
                    wait(dve, EX["up_mm"], s - 1)
                    V.tensor_copy(xT[:, v, :], X16[v]).then_inc(EX["xt_ready"], 1)
                if has(s, 1):
                    hidden(EX, s - 1, k)
                if has(s, 2):
                    copy_hT(EX, s - 2, v)
                if has(s, 1):
                    hidden_low(EX, s - 1, k)

            expert_pipeline(dve, estep)

            with dve.Fori(0, B - RING + 1, RING) as i:
                for r in range(RING):
                    b = i + r
                    dve.wait_ge(gath[r], 16 * TOPK + i * (16 * TOPK // RING))
                    xs = x_all[:, span(b * T, T)]
                    for k in range(TOPK):
                        n = V.scalar_tensor_tensor(xs, yg[:, r, k, :], wt_k[:, span(b * TOPK + k, 1)], xs, ALU.mult, ALU.add)
                        if k < TOPK - 1:
                            n.then_inc(S["acc_v"], 1)
                            dve.wait_ge(S["acc_v"], b * (TOPK - 1) + k + 1)
                        else:
                            n.then_inc(acc_done, 1)

        @block.gpsimd
        def _(pool):
            G = nc.gpsimd
            pool.wait_ge(par_in, 32)
            pool.wait_ge(S["aggr_done"], B)
            G.tensor_scalar(r1[:, :], mv1[:, :, 1:2].rearrange("p b c -> p (b c)"), EPS, None, ALU.add).then_inc(S["r1_eps"], 1)
            pool.wait_ge(S["r1_eps"], 1)
            G.tensor_tensor(r1[:, :], r1[:, :], c("half"), ALU.pow).then_inc(S["r1_done"], 1)
            pool.wait_ge(ctx_in_s, 16)
            half = c("half")[:, 0:1]
            for s in range(STEPS + 1):
                if does(s, 0):
                    b = s
                    pool.wait_ge(S["xn_ready"], b + 1)
                    xs = x_all[:, b * T:(b + 1) * T]
                    G.tensor_tensor(xs, xs, ctx_all[:, b * T:(b + 1) * T], ALU.add).then_inc(S["xc_ready"], 1)
                if does(s, 1):
                    b = s - 1
                    j = b % 2
                    pool.wait_ge(S["vneg_ready"], b + 1)
                    wait(pool, S["hpre_ready"], b - 1)
                    G.tensor_scalar(vpos[:, j:j + 1], vneg[:, j:j + 1], -1.0, EPS, ALU.mult, ALU.add).then_inc(S["v_done"], 1)
                    pool.wait_ge(S["v_done"], b + 1)
                    G.tensor_tensor(trs[:, j:j + 1], vpos[:, j:j + 1], half, ALU.pow).then_inc(S["trs_ready"], 1)
                    pool.wait_ge(S["mv2_ready"], b + 1)
                    wait(pool, S["xn2_ready"], b - 1)
                    G.tensor_scalar(v2[:, j:j + 1], mv2[:, j, 1:2], EPS, None, ALU.add).then_inc(S["v2_done"], 1)
                    pool.wait_ge(S["v2_done"], b + 1)
                    G.tensor_tensor(r2[:, j:j + 1], v2[:, j:j + 1], half, ALU.pow).then_inc(S["r2_ready"], 1)
                if s >= 6:
                    b = s - 6
                    if b % 4 == 0:
                        pool.wait_ge(S["slot_ready"], b + 4)
                    for k in range(TOPK):
                        G.indirect_dma_start(scatter_rows, bass.IndirectOffsetOnAxis(ap=slot_k[:, b * TOPK + k:b * TOPK + k + 1], axis=0),
                                             rows_all[:, b * 2 * T:(b + 1) * 2 * T], None).then_inc(S["scattered"], 16)
            for b in range(STEPS + 1 - 6, B):
                if b % 4 == 0:
                    pool.wait_ge(S["slot_ready"], b + 4)
                for k in range(TOPK):
                    G.indirect_dma_start(scatter_rows, bass.IndirectOffsetOnAxis(ap=slot_k[:, b * TOPK + k:b * TOPK + k + 1], axis=0),
                                         rows_all[:, b * 2 * T:(b + 1) * 2 * T], None).then_inc(S["scattered"], 16)

            def write_tile(t, j):
                pool.wait_ge(EX["y_ready"], t + 1)
                pool.dma_start(slot_y[span(t * P, P), :], y_sb[:, j, :]).then_inc(y_out[j], 16)

            with pool.Fori(0, NT - 1, 2) as t:
                write_tile(t, 0)
                write_tile(t + 1, 1)

            for j in range(2):
                pool.wait_ge(y_out[j], 8 * NT)
            pool.wait_ge(S["yslot_ready"], 1)
            for b in range(B):
                r = b % RING
                wait(pool, acc_done, b - RING + 1)
                for k in range(TOPK):
                    G.indirect_dma_start(yg[:, r, k, :], None, slot_y,
                                         bass.IndirectOffsetOnAxis(ap=yslot_k[:, b * TOPK + k:b * TOPK + k + 1], axis=0)).then_inc(gath[r], 16)


def constants():
    k = np.arange(P)
    tile = lambda a: np.broadcast_to(np.asarray(a, np.float32).reshape(1, -1), (P, np.asarray(a).size))
    g = np.arange(NG)
    return {
        "ident": np.eye(P, dtype=np.float32),
        "mean": np.full((P, P), 1.0 / P, np.float32),
        "lower": tile(g[None, :] < g[:, None]),
        "rank": tile(np.repeat(np.arange(1, TOPK + 1), NE)),
        "carry": tile(np.tile(np.arange(NE) > 0, 4)),
        "base": tile(np.arange(NE) * REGION),
        "tau": tile(np.arange(NT)),
        "half": np.full((P, NE), -0.5, np.float32),
    }, np.concatenate([np.eye(P), k[:, None] < k[None, :], np.ones((P, P))], 1).astype(np.float16)


def kernel(x, ctx_2048, L0_xattn_theta_w, L0_xattn_theta_b, L0_xattn_phi_w, L0_xattn_phi_b, L0_xattn_g_w,
           L0_xattn_g_b, L0_xattn_ln_gamma, L0_xattn_ln_beta, L0_xattn_out_w, L0_xattn_out_b, L0_ffn_Wg,
           L0_ffn_W1, L0_ffn_W3, L0_ffn_W2, L0_ffn_Ws1, L0_ffn_Ws3, L0_ffn_Ws2):
    import concourse.bacc as bacc
    from concourse.bass_utils import run_bass_kernel_spmd

    f = lambda a: np.asarray(a)
    consts, halves = constants()

    def rows(a):
        full = np.zeros((P, a.shape[1]), np.float32)
        full[:a.shape[0]] = a
        return full

    latent = lambda a: f(a).T.reshape(2, P, L).transpose(1, 0, 2).reshape(P, 2 * L)
    consts.update({
        "gamma": latent(L0_xattn_ln_gamma), "beta": latent(L0_xattn_ln_beta),
        "gb": np.broadcast_to(np.tile(f(L0_xattn_g_b), 2), (P, 2 * L)),
        "thw": f(L0_xattn_theta_w).T, "phw": f(L0_xattn_phi_w).T, "gw": f(L0_xattn_g_w).T,
        "wg": f(L0_ffn_Wg).T.reshape(2, P, NE).transpose(1, 0, 2).reshape(P, 2 * NE),
        "outw": rows(f(L0_xattn_out_w).T), "outb": f(L0_xattn_out_b).reshape(P, 1),
        "thb": rows(f(L0_xattn_theta_b).reshape(L, 1)), "phb": rows(f(L0_xattn_phi_b).reshape(L, 1)),
    })
    params = np.concatenate([consts[n] for n in COLS], 1)
    assert params.shape == (P, NCOLS)

    w1 = np.concatenate([f(L0_ffn_W1), f(L0_ffn_Ws1).reshape(2, NF, T)])
    w3 = np.concatenate([f(L0_ffn_W3), f(L0_ffn_Ws3).reshape(2, NF, T)])
    w2 = np.concatenate([f(L0_ffn_W2), f(L0_ffn_Ws2).reshape(T, 2, NF).transpose(1, 0, 2)])
    w13 = np.concatenate([w1, w3], 1).transpose(0, 2, 1).reshape(NU, 2, P, UP1).transpose(0, 2, 1, 3).reshape(NU, P, 2 * UP1)
    w2 = w2.transpose(0, 2, 1).reshape(NU, 2, FC, T).transpose(0, 2, 1, 3).reshape(NU, FC, 2 * T)

    arrays = {"x_dram": f(x), "ctx_dram": f(ctx_2048), "params_dram": params, "halves_dram": halves,
              "w13_dram": w13, "w2_dram": w2}
    arrays = {n: np.ascontiguousarray(a) for n, a in arrays.items()}
    nc = bacc.Bacc("TRN2", target_bir_lowering=False, num_devices=1)
    args = [nc.dram_tensor(n, a.shape, mybir.dt.from_np(a.dtype), kind="ExternalInput").ap() for n, a in arrays.items()]
    out = nc.dram_tensor("out_dram", (B, P, T), F32, kind="ExternalOutput").ap()
    build(nc, *args, out)
    r = run_bass_kernel_spmd(nc, [arrays], core_ids=[0])
    return r.results[0]["out_dram"]
```

```python
from contextlib import ExitStack

import numpy as np

import concourse.bass as bass
from concourse import mybir

ALU = mybir.AluOpType
ACT = mybir.ActivationFunctionType
AX = mybir.AxisListType
F32 = mybir.dt.float32
F16 = mybir.dt.float16
I32 = mybir.dt.int32
U32 = mybir.dt.uint32

P = 128
B = 16
T = 256
L = 64
NE = 16
NU = NE + 2
NF = 176
FC = NF // 2
NG = 4
TOPG = 2
TOPK = 4
EPS = 1e-5
WS = 64.0
REGION = B * P + P
NT = (B * P * TOPK + NE * (P - 1)) // P + 1
NT += -NT % 8
SLOTS = NE * REGION
UP1 = 2 * NF
W13 = 2 * 2 * UP1
W2 = 2 * 2 * T
WU = W13 + W2
ROW32 = T + NE + 1
ROW = 2 * ROW32
TOKENS = B * P

COLS = {}
_at = 0
for _n, _w in (("ident", P), ("mean", P), ("lower", NG * NG), ("rank", TOPK * NE), ("carry", 4 * NE),
               ("base", NE), ("token", B), ("pad", 1), ("tau", NT), ("half", NE), ("gamma", 2 * L), ("beta", 2 * L), ("gb", 2 * L),
               ("thw", L), ("phw", L), ("gw", L), ("wg", 2 * NE), ("outw", P), ("outb", 1), ("thb", 1), ("phb", 1)):
    COLS[_n] = (_at, _at + _w)
    _at += _w
NCOLS = _at


def build(nc, x, ctx_in, params, halves, w13_in, w2_in, out):
    scatter_rows = nc.dram_tensor("slot_rows", (SLOTS + P, ROW32), F32, kind="Internal").ap()
    sums = [nc.dram_tensor(f"sums{j}", (TOKENS + P, T), F32, kind="Internal").ap() for j in range(2)]

    with ExitStack() as stack:
        def sb(name, shape, dt=F32):
            return stack.enter_context(nc.sbuf_tensor(name, shape, dt))

        def sem(name):
            return stack.enter_context(nc.semaphore(name))

        def span(at, n):
            return slice(at, at + n) if isinstance(at, int) else bass.ds(at, n)

        def wait(eng, s, n):
            if not isinstance(n, int) or n > 0:
                eng.wait_ge(s, n)

        def own_wait(eng):
            eng.nop(nofuse=True)

        par = sb("par", [P, NCOLS])
        hal = sb("hal", [P, 3 * P], F16)
        ident16, tri16, ones16 = hal[:, 0:P], hal[:, P:2 * P], hal[:, 2 * P:3 * P]

        def c(name, rows=P):
            a, b = COLS[name]
            return par[0:rows, a:b]

        x_all = sb("x_all", [P, B * T])
        ctx_all = sb("ctx_all", [P, B * T])
        rows32 = sb("rows_all", [P, B * ROW32])
        rows_all = rows32[:, :].bitcast(F16)
        xT_all = sb("xT_all", [P, B * 4 * P], F16)
        w = sb("w", [P, NU * WU], F16)
        wst13 = sb("wst13", [P, 2, 2 * UP1])
        wst2 = sb("wst2", [FC, 2, 2 * T])
        wg16 = sb("wg16", [P, 2, 2 * NE], F16)
        st1 = sb("st1", [P, B, 6])
        mv1 = sb("mv1", [P, B, 2])
        r1 = sb("r1", [P, B])
        xn = sb("xn", [P, 2, T])
        th = sb("th", [L, 2, T])
        ph = sb("ph", [L, 2, T])
        g_sb = sb("g_sb", [P, 2, 2 * L])
        nmax = sb("nmax", [P, 2, 2])
        psums = sb("psums", [P, 2, 2])
        rsum = sb("rsum", [P, 2, 2])
        p_sb = sb("p_sb", [P, 2, 2 * T])
        pT = sb("pT", [P, 2, 2 * T])
        tx = sb("tx", [P, 2, 2 * L])
        tst = sb("tst", [P, 2, 6])
        tmv = sb("tmv", [P, 2, 2])
        gmv = sb("gmv", [P, 2, 2])
        vneg = sb("vneg", [P, 2])
        vpos = sb("vpos", [P, 2])
        trs = sb("trs", [P, 2])
        hc = sb("hc", [P, 2, 2 * L])
        hpre = sb("hpre", [P, 2, 2 * L])
        hr = sb("hr", [L, 2, T])
        st2 = sb("st2", [P, 2, 6])
        mv2 = sb("mv2", [P, 2, 2])
        v2 = sb("v2", [P, 2])
        r2 = sb("r2", [P, 2])
        xn2 = sb("xn2", [P, 2, T])
        Q = 4
        lg = sb("lg", [P, Q * NE])
        qm = sb("qm", [P, Q])
        qs = sb("qs", [P, Q])
        qr = sb("qr", [P, Q])
        qz = sb("qz", [P, Q * NE])
        qe = sb("qe", [P, Q * NE])
        score = sb("score", [P, Q * NE])
        gmax = sb("gmax", [P, Q * NG])
        gcmp = sb("gcmp", [P, Q * NG * NG])
        geq = sb("geq", [P, Q * NG * NG])
        grank = sb("grank", [P, Q * NG])
        gsel = sb("gsel", [P, Q * NG])
        gsub = sb("gsub", [P, Q * NG])
        masked = sb("masked", [P, Q * NE])
        top8 = sb("top8", [P, Q * 8])
        repl = sb("repl", [P, Q * NE])
        sel = sb("sel", [P, Q * NE])
        diff = sb("diff", [P, Q * NE])
        sel16 = sb("sel16", [P, Q * NE], F16)
        cum = sb("cum", [P, Q * NE])
        base = sb("base", [P, NE])
        pad_rows = sb("pad_rows", [P, ROW32])
        zero_sum = sb("zero_sum", [P, T])
        slot = sb("slot", [P, Q * NE])
        onek = sb("onek", [P, Q * TOPK * NE])
        onev = sb("onev", [P, Q * TOPK * NE])
        slot_f = sb("slot_f", [P, B * TOPK])
        slot_k = sb("slot_k", [P, B * TOPK], U32)
        cnt = sb("cnt", [P, NE])
        cnt_i = sb("cnt_i", [P, NE], I32)
        nt_a = sb("nt_a", [P, NE])
        nt_i = sb("nt_i", [P, NE], I32)
        nt_s = sb("nt_s", [P, NE], I32)
        nt_f = sb("nt_f", [P, NE])
        ntc = sb("ntc", [P, NE])
        te = sb("te", [1, NT])
        tst0 = sb("tst0", [1, NT])
        trow = sb("trow", [1, NT])
        tval = sb("tval", [1, NT])
        row_i = sb("row_i", [1, NT], I32)
        exp_e = sb("exp_e", [1, NT], I32)
        exp_i = sb("exp_i", [1, NT], I32)
        silu = sb("silu", [P, 2, NF])
        hid = sb("hid", [P, 2, NF])
        hh = sb("hh", [P, 2, 2 * NF], F16)
        hT = sb("hT", [FC, 2, 4 * P], F16)
        m = NT * NE
        ind, indc = ctx_all[0:1, 0:m], ctx_all[0:1, m:2 * m]
        RING = 4
        META = NE + 1
        _at = [0]

        def reuse(n):
            _at[0] += n
            assert _at[0] <= B * T
            return ctx_all[:, _at[0] - n:_at[0]]

        meta = reuse(NT * META)
        xg32 = reuse(RING * ROW32)
        xg = xg32.bitcast(F16).rearrange("p (j c) -> p j c", j=RING)
        xg32 = xg32.rearrange("p (j c) -> p j c", j=RING)
        xT = reuse(2 * 2 * P).bitcast(F16).rearrange("p (j c) -> p j c", j=2)
        y_sb = reuse(2 * T).rearrange("p (j c) -> p j c", j=2)
        part = xT_all[:, :].bitcast(F32).rearrange("p (j b t) -> p j b t", j=2, t=T)
        idx = sb("idx", [P, 2], U32)

        bank = [stack.enter_context(nc.psum_tensor(f"bank{i}", [P, 512], F32)) for i in range(8)]
        TP, GP, SP_, PT, TS, HO, XB, LB = [b[:, :] for b in bank]
        XB16 = XB.bitcast(F16)[:, 0:4 * P]

        par_in, ctx_in_s, wst_in0, wst_in1 = sem("par_in"), sem("ctx_loaded"), sem("wst_in0"), sem("wst_in1")
        x_in = [sem(f"x_in{i}") for i in range(4)]
        wst_in = [wst_in0, wst_in1]
        names = ("stat_done aggr_done r1_eps r1_done wg_hi wg_lo base_set xn_ready xc_ready th_mm ph_mm thph_ready g_mm g_ready s_mm max_ready "
                 "p_ready pt_mm pt_ready rs_ready t_mm tx_ready ts_done ta_done tmv_ready st_mm gmv_done vneg_ready "
                 "v_done trs_ready hc_done hpre_ready ht_mm hr_ready o_mm xr_ready st2_done mv2_ready v2_done "
                 "r2_ready xn2_ready hi_ready lo_ready xt_mm xt_ready l_mm lg_ready wh_ready wl_ready "
                 "route_max route_z route_e route_sum route_recip route_score group_max group_cmp group_eq group_before "
                 "group_rank group_chosen mask_mult masked top_values top_four top_replaced chosen_diff chosen rank_scan "
                 "rank one_hot weights_set slots slots_by_rank slots_sum sel_ready pre_mm pre_read slot_ready scattered zero_set counts_ready "
                 "table_v table_ready tails_in gathered_all out_written acc_v sums_zero meta_set idx_set hidden_used").split()
        S = {n: sem(n) for n in names}
        part_in = [sem(f"part_in{n}") for n in range(2)]
        acc_done = sem("acc_done")

        FFN = "xt_mm xt_ready up_mm silu_ready h_ready hhi_ready hlo_ready ht_mm hT_ready dn_mm y_ready".split()
        SH = {n: sem(f"sh_{n}") for n in FFN}
        EX = {n: sem(f"ex_{n}") for n in FFN}

        LAG = {"xg_in": 0, "xt_ready": 1, "hlo_ready": 3, "hT_ready": 3}
        RS = {n: [sem(f"ex_{n}{m}") for m in range(RING)] for n in LAG}

        def ring_count(name, t, rel=None):
            if isinstance(t, int):
                return 16 * (t // RING + 1) + (16 if t % RING >= RING - LAG[name] else 0)
            m = rel % RING
            return 4 * (t - m) + 16 + (16 if m >= RING - LAG[name] else 0)

        y_out = [sem("y_out0"), sem("y_out1")]

        FIRST = 8
        STEPS = B + 10
        AFTER_COUNT = 4

        def pipeline(eng, step):
            for s in range(FIRST):
                step(s, s % 4)
            with eng.Fori(FIRST, B - 3, 4) as i:
                for v in range(4):
                    step(i + v, v)
            for s in range(B, STEPS):
                step(s, s % 4)

        def tile(s, v, lag, part, count=B):
            if not isinstance(s, int) or 0 <= s - lag < count:
                part(s - lag, (v - lag) % 4)

        def group(s, v, lag, part):
            if (v - lag) % 4 == 0 and (not isinstance(s, int) or 0 <= s - lag < B):
                part(s - lag)

        def expert_pipeline(eng, step, lags=3):
            for s in range(2 * RING):
                step(s, s % RING, None)
            with eng.Fori(2 * RING, NT - 2 * RING + 1, 2 * RING) as i:
                for v in range(2 * RING):
                    if v % RING == 0:
                        r = eng.snap(4 * (i + v) + 16)
                    step(i + v, v, r)
            for s in range(NT, NT + lags):
                step(s, s % RING, None)

        def has(s, lag):
            return not isinstance(s, int) or 0 <= s - lag < NT

        def shared_pipeline(eng, step):
            for b in range(2):
                for u in range(2):
                    step(b, u)
            with eng.Fori(2, B) as b:
                for u in range(2):
                    step(b, u)
            for u in range(2):
                step(B, u)

        def shared(n, lag):
            return not isinstance(n, int) or 0 <= n - lag < 2 * B

        U, H, Y = [TP, GP], [SP_, PT], [TS, HO]
        X16 = [b.bitcast(F16)[:, 0:4 * P] for b in (XB, LB)]
        H16 = [h.bitcast(F16)[0:FC, 0:4 * P] for h in H]

        block = stack.enter_context(nc.Block())

        @block.sync
        def _(sp):
            sp.dma_start(par[:, :], params).then_inc(par_in, 16)
            sp.dma_start(hal[:, :], halves).then_inc(par_in, 16)
            xv = x.rearrange("b p t -> p b t")
            cv = ctx_in.rearrange("b p t -> p b t")
            x3 = x_all[:, :].rearrange("p (b t) -> p b t", t=T)
            c3 = ctx_all[:, :].rearrange("p (b t) -> p b t", t=T)
            for n in range(4):
                sp.dma_start(x3[:, 4 * n:4 * n + 4, :], xv[:, 4 * n:4 * n + 4, :]).then_inc(x_in[n], 16)
            sp.dma_start(c3, cv).then_inc(ctx_in_s, 16)

            def load_weights(e, j):
                wait(sp, S["wl_ready"], e - 1)
                sp.dma_start(wst13[:, j, :], w13_in[span(e, 1), :, :].rearrange("a p f -> (a p) f")).then_inc(wst_in[j], 16)
                sp.dma_start(wst2[:, j, :], w2_in[span(e, 1), :, :].rearrange("a p f -> (a p) f")).then_inc(wst_in[j], 16)

            for e in range(2):
                load_weights(e, e)
            with sp.Fori(2, NU - 1, 2) as e:
                load_weights(e, 0)
                load_weights(e + 1, 1)

            sp.wait_ge(S["zero_set"], 1)
            for j in range(2):
                sp.dma_start(sums[j].rearrange("(b p) t -> p b t", p=P),
                             zero_sum[:, :].unsqueeze(1).broadcast_to([P, B + 1, T])).then_inc(S["sums_zero"], 16)

            sp.dma_start(scatter_rows[SLOTS:SLOTS + P, :], pad_rows[:, :]).then_inc(S["tails_in"], 16)
            sp.wait_ge(S["counts_ready"], 1)
            with sp.Fori(0, NE) as e:
                n = sp.value_load(cnt_i[0:1, span(e, 1)], min_val=0, max_val=TOKENS)
                sp.dma_start(scatter_rows[bass.ds(e * REGION + n, P), :], pad_rows[:, :]).then_inc(S["tails_in"], 16)

            sp.wait_ge(S["tails_in"], 16 * (NE + 1))
            sp.wait_ge(S["scattered"], 16 * B * TOPK)
            sp.wait_ge(S["table_ready"], 1)

            def load_tile(t, v):
                if not isinstance(t, int) or t >= RING:
                    sp.wait_ge(RS["xt_ready"][v], ring_count("xt_ready", t - RING, v))
                r = sp.value_load(row_i[0:1, span(t, 1)], min_val=0, max_val=SLOTS)
                sp.dma_start(xg32[:, v, :], scatter_rows[bass.ds(r, P), :]).then_inc(RS["xg_in"][v], 16)

            for t in range(RING):
                load_tile(t, t)
            with sp.Fori(RING, NT - RING + 1, RING) as t:
                for v in range(RING):
                    load_tile(t + v, v)

            for j in range(2):
                sp.wait_ge(y_out[j], 8 * NT)
            sv = [a[0:TOKENS, :].rearrange("(b p) t -> p b t", p=P) for a in sums]
            ov = out.rearrange("b p t -> p b t")
            CB = 4
            for n in range(B // CB):
                for j in range(2):
                    if n >= 2:
                        sp.wait_ge(acc_done, n - 1)
                    sp.dma_start(part[:, j, CB * (n % 2):CB * (n % 2) + CB, :], sv[j][:, CB * n:CB * n + CB, :]).then_inc(part_in[n % 2], 16)
            for n in range(B // CB):
                sp.wait_ge(acc_done, n + 1)
                sp.dma_start(ov[:, CB * n:CB * n + CB, :],
                             x_all[:, CB * n * T:CB * (n + 1) * T].rearrange("p (b t) -> p b t", t=T)).then_inc(S["out_written"], 16)
            sp.wait_ge(S["out_written"], 16 * B // CB)

        @block.scalar
        def _(act):
            A = nc.scalar.activation
            act.wait_ge(par_in, 32)

            def weights_high(s, u):
                j = u % 2
                act.wait_ge(wst_in[j], 16 * s + 32 - 16 * j)
                A(w[:, span(s * WU, 2 * UP1)], wst13[:, j, :], ACT.Copy, scale=WS)
                A(w[0:FC, span(s * WU + W13, 2 * T)], wst2[:, j, :], ACT.Copy, scale=WS).then_inc(S["wh_ready"], 1)

            def theta_phi(b, u):
                j = u % 2
                act.wait_ge(S["th_mm"], b + 1)
                act.wait_ge(S["ph_mm"], b + 1)
                wait(act, S["s_mm"], b - 1)
                A(th[:, j, :], TP[0:L, 0:T], ACT.Identity, bias=c("thb", L))
                A(ph[:, j, :], TP[0:L, T:2 * T], ACT.Identity, bias=c("phb", L)).then_inc(S["thph_ready"], 1)

            def exps(b, u):
                j = u % 2
                act.wait_ge(S["max_ready"], b + 1)
                wait(act, S["pt_mm"], b - 1)
                wait(act, S["rs_ready"], b - 1)
                for h in range(2):
                    i = A(p_sb[:, j, h * T:(h + 1) * T], SP_[:, h * T:(h + 1) * T], ACT.Exp,
                          bias=nmax[:, j, h:h + 1], accum_out=psums[:, j, h:h + 1])
                i.then_inc(S["p_ready"], 1)

            def copy_pT(b, u):
                j = u % 2
                act.wait_ge(S["pt_mm"], b + 1)
                wait(act, S["t_mm"], b - 1)
                A(pT[:, j, :], PT, ACT.Copy).then_inc(S["pt_ready"], 1)

            def relu(b, u):
                j = u % 2
                act.wait_ge(S["ht_mm"], b + 1)
                wait(act, S["o_mm"], b - 1)
                A(hr[:, j, :], HO[0:L, 0:T], ACT.Relu).then_inc(S["hr_ready"], 1)

            def high(b, u):
                j = u % 2
                act.wait_ge(S["xn2_ready"], b + 1)
                A(rows_all[:, span(b * ROW, T)], xn2[:, j, :], ACT.Copy).then_inc(S["hi_ready"], 1)

            def route_exp(b0):
                act.wait_ge(S["route_z"], b0 + 4)
                A(qe[:, :], qz[:, :], ACT.Exp).then_inc(S["route_e"], 4)

            def step(s, v):
                tile(s, v, 3, high)
                tile(s, v, 1, weights_high, count=NU)
                tile(s, v, 1, exps)
                tile(s, v, 2, relu)
                group(s, v, 6, route_exp)
                tile(s, v, 1, copy_pT)
                tile(s, v, 0, theta_phi)
            pipeline(act, step)

            def gate(G, n, j):
                act.wait_ge(G["up_mm"], n + 1)
                A(silu[:, j, :], U[j][:, 0:NF], ACT.Silu, scale=1 / WS).then_inc(G["silu_ready"], 1)

            def hidden_high(G, n, j):
                act.wait_ge(G["h_ready"], n + 1)
                wait(act, G["ht_mm"], n - 1)
                A(hh[:, j, 0:NF], hid[:, j, :], ACT.Copy).then_inc(G["hhi_ready"], 1)

            def sstep(b, u):
                n = 2 * b + u
                if shared(n, 0):
                    gate(SH, n, u)
                    hidden_high(SH, n, u)

            shared_pipeline(act, sstep)

            def estep(s, v, r):
                v %= RING
                k = (v + 1) % 2
                if has(s, 1):
                    gate(EX, s - 1, k)
                if has(s, 1):
                    hidden_high(EX, s - 1, k)
                if has(s, 3):
                    t = s - 3
                    e = act.value_load(exp_e[0:1, span(t, 1)], min_val=0, max_val=NE - 1)
                    act.wait_ge(EX["dn_mm"], t + 1)
                    wait(act, y_out[k], 8 * (t - k))
                    A(y_sb[:, k, :], Y[k][:, 0:T], ACT.Copy, scale=meta[:, span(t * META + e, 1)]).then_inc(EX["y_ready"], 1)

            expert_pipeline(act, estep)

        @block.tensor
        def _(pe):
            mm, tr = nc.tensor.matmul, nc.tensor.transpose
            ident = c("ident")
            pe.wait_ge(par_in, 32)
            pe.wait_ge(ctx_in_s, 16)

            def theta(b, u):
                wait(pe, S["thph_ready"], b)
                mm(TP[0:L, 0:T], c("thw"), ctx_all[:, span(b * T, T)], start=True, stop=True).then_inc(S["th_mm"], 1)

            def phi(b, u):
                pe.wait_ge(S["xn_ready"], b + 1)
                mm(TP[0:L, T:2 * T], c("phw"), xn[:, u % 2, :], start=True, stop=True).then_inc(S["ph_mm"], 1)

            def project_g(b, u):
                pe.wait_ge(S["xn_ready"], b + 1)
                wait(pe, S["g_ready"], b)
                for h in range(2):
                    i = mm(GP[:, h * L:(h + 1) * L], xn[:, u % 2, h * P:(h + 1) * P], c("gw"), start=True, stop=True)
                i.then_inc(S["g_mm"], 1)

            def scores(b, u):
                j = u % 2
                pe.wait_ge(S["thph_ready"], b + 1)
                wait(pe, S["p_ready"], b)
                for h in range(2):
                    i = mm(SP_[:, h * T:(h + 1) * T], th[:, j, h * P:(h + 1) * P], ph[:, j, :], start=True, stop=True)
                i.then_inc(S["s_mm"], 1)

            def transpose_p(b, u):
                j = u % 2
                pe.wait_ge(S["p_ready"], b + 1)
                wait(pe, S["pt_ready"], b)
                for h in range(2):
                    for k in range(2):
                        i = tr(PT[:, k * T + h * P:k * T + h * P + P], p_sb[:, j, h * T + k * P:h * T + k * P + P], ident)
                i.then_inc(S["pt_mm"], 1)

            def attend(b, u):
                j = u % 2
                pe.wait_ge(S["pt_ready"], b + 1)
                pe.wait_ge(S["g_ready"], b + 1)
                wait(pe, S["gmv_done"], b)
                for h in range(2):
                    for k in range(2):
                        i = mm(TS[:, h * L:(h + 1) * L], pT[:, j, k * T + h * P:k * T + h * P + P],
                               g_sb[:, j, k * L:(k + 1) * L], start=k == 0, stop=k == 1)
                i.then_inc(S["t_mm"], 1)

            def mean_all(b, u):
                j = u % 2
                pe.wait_ge(S["tmv_ready"], b + 1)
                mm(TS[:, 2 * L:2 * L + 2], c("mean"), tmv[:, j, :], start=True, stop=True).then_inc(S["st_mm"], 1)

            def transpose_h(b, u):
                j = u % 2
                pe.wait_ge(S["hpre_ready"], b + 1)
                wait(pe, S["xr_ready"], b)
                own_wait(pe)
                for h in range(2):
                    i = tr(HO[0:L, h * P:(h + 1) * P], hpre[:, j, h * L:(h + 1) * L], ident)
                i.then_inc(S["ht_mm"], 1)

            def project_out(b, u):
                j = u % 2
                pe.wait_ge(S["hr_ready"], b + 1)
                mm(HO[:, T:2 * T], c("outw", L), hr[:, j, :], start=True, stop=True).then_inc(S["o_mm"], 1)

            def transpose_rows(b, u):
                pe.wait_ge(S["lo_ready"], b + 1)
                wait(pe, S["xt_ready"], b)
                for k in range(4):
                    i = tr(XB16[:, k * P:(k + 1) * P], rows_all[:, span(b * ROW + k * P, P)], ident16)
                i.then_inc(S["xt_mm"], 1)

            def router(b, u):
                pe.wait_ge(S["xt_ready"], b + 1)
                wait(pe, S["lg_ready"], b)
                if u == AFTER_COUNT % 4 and (not isinstance(b, int) or b >= AFTER_COUNT):
                    pe.wait_ge(S["pre_read"], b - AFTER_COUNT + 4)
                for k in range(4):
                    for w in range(2):
                        i = mm(LB[:, u * NE:(u + 1) * NE], xT_all[:, span((b * 4 + k) * P, P)],
                               wg16[:, k % 2, w * NE:(w + 1) * NE], start=k == 0 and w == 0, stop=k == 3 and w == 1)
                i.then_inc(S["l_mm"], 1)

            def count(b0):
                pe.wait_ge(S["sel_ready"], b0 + 4)
                pe.wait_ge(S["lg_ready"], min(b0 + AFTER_COUNT, B) if isinstance(b0, int) else b0 + AFTER_COUNT)
                for u in range(4):
                    for v in range(u + 1):
                        mm(LB[:, 64 + u * NE:64 + (u + 1) * NE], tri16 if v == u else ones16,
                           sel16[:, v * NE:(v + 1) * NE], start=v == 0, stop=v == u)
                for v in range(4):
                    i = mm(LB[:, 128:128 + NE], ones16, sel16[:, v * NE:(v + 1) * NE], start=v == 0, stop=v == 3)
                i.then_inc(S["pre_mm"], 4)

            def step(s, v):
                tile(s, v, 0, theta)
                tile(s, v, 2, transpose_h)
                tile(s, v, 3, router)
                tile(s, v, 1, transpose_p)
                tile(s, v, 2, project_out)
                tile(s, v, 1, attend)
                tile(s, v, 0, phi)
                tile(s, v, 0, project_g)
                tile(s, v, 1, mean_all)
                tile(s, v, 0, scores)
                tile(s, v, 2, transpose_rows)
                group(s, v, 6, count)
            pipeline(pe, step)

            def up(done, j, xt, wcol):
                for k in range(2):
                    for wpart, part in ((0, 0), (0, 1), (1, 0)):
                        i = mm(U[j][:, 0:UP1], xt(2 * part + k), w[:, span(wcol + (2 * wpart + k) * UP1, UP1)],
                               start=k == 0 and (wpart, part) == (0, 0), stop=k == 1 and wpart == 1)
                i.then_inc(done, 1)

            def transpose_hidden(done, j):
                for k in range(4):
                    i = tr(H16[j][:, k * P:(k + 1) * P], hh[:, j, k * FC:(k + 1) * FC], ident16)
                i.then_inc(done, 1)

            def down(done, j, y, wcol, start, stop):
                for k in range(2):
                    for wpart, part in ((0, 0), (0, 1), (1, 0)):
                        i = mm(y[:, 0:T], hT[:, j, (2 * part + k) * P:(2 * part + k + 1) * P],
                               w[0:FC, span(wcol + W13 + (2 * wpart + k) * T, T)],
                               start=start and k == 0 and (wpart, part) == (0, 0), stop=stop and k == 1 and wpart == 1)
                i.then_inc(done, 1)

            pe.wait_ge(S["wl_ready"], NU)
            for n in ("thph_ready", "g_ready", "p_ready", "pt_ready", "gmv_done", "xr_ready", "xt_ready", "pre_read"):
                pe.wait_ge(S[n], B)

            def sstep(b, u):
                n = 2 * b + u
                if shared(n, 0):
                    wait(pe, SH["h_ready"], n - 1)
                    up(SH["up_mm"], u, lambda k: xT_all[:, span((b * 4 + k) * P, P)], (NE + u) * WU)
                if shared(n, 1):
                    pe.wait_ge(SH["hlo_ready"], n)
                    wait(pe, SH["hT_ready"], n - 2)
                    transpose_hidden(SH["ht_mm"], 1 - u)
                if shared(n, 2):
                    if u == 0:
                        wait(pe, SH["y_ready"], b - 1)
                    pe.wait_ge(SH["hT_ready"], n - 1)
                    down(SH["dn_mm"], u, Y[0], (NE + u) * WU, start=u == 0, stop=u == 1)

            shared_pipeline(pe, sstep)

            pe.wait_ge(S["table_ready"], 1)
            pe.wait_ge(SH["y_ready"], B)

            up_weights = {}

            def estep(s, step_v, r):
                v = step_v % RING
                k = (v + 1) % 2

                def ready(name, lag):
                    t = s - lag
                    pe.wait_ge(RS[name][(v - lag) % RING], ring_count(name, t) if r is None else r)

                if has(s, 3):
                    ready("hlo_ready", 3)
                    transpose_hidden(EX["ht_mm"], k)
                if has(s, 1):
                    e = pe.value_load(exp_i[0:1, span(s - 1, 1)], min_val=0, max_val=(NE - 1) * WU)
                    up_weights[step_v] = e
                    ready("xt_ready", 1)
                    up(EX["up_mm"], k, lambda q: xT[:, k, q * P:(q + 1) * P], e)
                if has(s, 0):
                    ready("xg_in", 0)
                    for q in range(4):
                        i = tr(X16[v % 2][:, q * P:(q + 1) * P], xg[:, v, q * P:(q + 1) * P], ident16)
                    i.then_inc(EX["xt_mm"], 1)
                if has(s, 3):
                    if r is not None and step_v >= 2:
                        e = up_weights[step_v - 2]
                    else:
                        e = pe.value_load(exp_i[0:1, span(s - 3, 1)], min_val=0, max_val=(NE - 1) * WU)
                    ready("hT_ready", 3)
                    if r is None and s >= NT:
                        pe.wait_ge(EX["y_ready"], s - 4)
                    down(EX["dn_mm"], k, Y[k], e, start=True, stop=True)

            expert_pipeline(pe, estep)

        @block.vector
        def _(dve):
            V = nc.vector
            rows3d = rows32[:, :].rearrange("p (b c) -> p b c", c=ROW32)
            rows3 = lambda a, n: a[:, :].rearrange("p (q e) -> p q e", e=n)

            for b in range(B):
                if b % 4 == 0:
                    dve.wait_ge(x_in[b // 4], 16)
                V.bn_stats(st1[:, b, :], x_all[:, b * T:(b + 1) * T]).then_inc(S["stat_done"], 1)
            for b in range(B):
                dve.wait_ge(S["stat_done"], b + 1)
                V.bn_aggr(mv1[:, b, :], st1[:, b, :]).then_inc(S["aggr_done"], 1)
            dve.wait_ge(par_in, 32)
            for name, lag in LAG.items():
                for m in range(RING - lag, RING):
                    dve.sem_inc(RS[name][m], 16)
            V.memset(pad_rows[:, :], 0.0).then_inc(S["meta_set"], 1)
            V.memset(zero_sum[:, :], 0.0)
            V.tensor_copy(rows3d[:, :, ROW32 - 1:ROW32], c("token").unsqueeze(2))
            dve.wait_ge(S["meta_set"], 1)
            V.tensor_copy(pad_rows[:, ROW32 - 1:ROW32], c("pad")).then_inc(S["zero_set"], 1)
            V.tensor_scalar(wg16[:, :, 0:NE], c("wg").rearrange("p (k e) -> p k e", e=NE), WS, None, ALU.mult).then_inc(S["wg_hi"], 1)
            V.tensor_copy(base[:, :], c("base")).then_inc(S["base_set"], 1)
            dve.wait_ge(S["wg_hi"], 1)
            V.scalar_tensor_tensor(wg16[:, :, NE:2 * NE], c("wg").rearrange("p (k e) -> p k e", e=NE), WS,
                                   wg16[:, :, 0:NE], ALU.mult, ALU.subtract).then_inc(S["wg_lo"], 1)
            dve.wait_ge(S["r1_done"], 1)

            def normalise(b, u):
                j = u % 2
                wait(dve, S["g_mm"], b - 1)
                V.tensor_scalar(xn[:, j, :], x_all[:, span(b * T, T)], mv1[:, span(b, 1), 0:1].rearrange("p a c -> p (a c)"),
                                r1[:, span(b, 1)], ALU.subtract, ALU.mult).then_inc(S["xn_ready"], 1)

            def values(b, u):
                j = u % 2
                dve.wait_ge(S["g_mm"], b + 1)
                wait(dve, S["t_mm"], b - 1)
                V.tensor_tensor(g_sb[:, j, :], GP[:, 0:2 * L], c("gb"), ALU.add).then_inc(S["g_ready"], 1)

            def row_max(b, u):
                j = u % 2
                dve.wait_ge(S["s_mm"], b + 1)
                wait(dve, S["p_ready"], b - 1)
                V.tensor_reduce(nmax[:, j, :], SP_.rearrange("p (h t) -> p h t", h=2), AX.X, ALU.max, negate=True).then_inc(S["max_ready"], 1)

            def recip(b, u):
                j = u % 2
                dve.wait_ge(S["p_ready"], b + 1)
                V.reciprocal(rsum[:, j, :], psums[:, j, :]).then_inc(S["rs_ready"], 1)

            def attended(b, u):
                j = u % 2
                dve.wait_ge(S["rs_ready"], b + 1)
                dve.wait_ge(S["t_mm"], b + 1)
                V.tensor_tensor(tx[:, j, :].rearrange("p (h l) -> p h l", h=2), TS[:, 0:2 * L].rearrange("p (h l) -> p h l", h=2),
                                rsum[:, j, :].unsqueeze(2).broadcast_to([P, 2, L]), ALU.mult).then_inc(S["tx_ready"], 1)

            def latent_stats(b, u):
                dve.wait_ge(S["tx_ready"], b + 1)
                own_wait(dve)
                V.bn_stats(tst[:, u % 2, :], tx[:, u % 2, :]).then_inc(S["ts_done"], 1)

            def latent_aggr(b, u):
                dve.wait_ge(S["ts_done"], b + 1)
                own_wait(dve)
                V.bn_aggr(tmv[:, u % 2, :], tst[:, u % 2, :]).then_inc(S["ta_done"], 1)

            def latent_moments(b, u):
                j = u % 2
                dve.wait_ge(S["ta_done"], b + 1)
                V.scalar_tensor_tensor(tmv[:, j, 1:2], tmv[:, j, 0:1], tmv[:, j, 0:1], tmv[:, j, 1:2], ALU.mult, ALU.add).then_inc(S["tmv_ready"], 1)

            def latent_all(b, u):
                dve.wait_ge(S["st_mm"], b + 1)
                V.tensor_copy(gmv[:, u % 2, :], TS[:, 2 * L:2 * L + 2]).then_inc(S["gmv_done"], 1)

            def latent_var(b, u):
                j = u % 2
                dve.wait_ge(S["gmv_done"], b + 1)
                wait(dve, S["trs_ready"], b - 1)
                V.scalar_tensor_tensor(vneg[:, j:j + 1], gmv[:, j, 0:1], gmv[:, j, 0:1], gmv[:, j, 1:2],
                                       ALU.mult, ALU.subtract).then_inc(S["vneg_ready"], 1)

            def latent_centre(b, u):
                j = u % 2
                V.scalar_tensor_tensor(hc[:, j, :], tx[:, j, :], gmv[:, j, 0:1], c("gamma"), ALU.subtract, ALU.mult).then_inc(S["hc_done"], 1)

            def latent_out(b, u):
                j = u % 2
                dve.wait_ge(S["hc_done"], b + 1)
                dve.wait_ge(S["trs_ready"], b + 1)
                wait(dve, S["ht_mm"], b - 1)
                V.scalar_tensor_tensor(hpre[:, j, :], hc[:, j, :], trs[:, j:j + 1], c("beta"), ALU.mult, ALU.add).then_inc(S["hpre_ready"], 1)

            def residual(b, u):
                dve.wait_ge(S["o_mm"], b + 1)
                dve.wait_ge(S["xc_ready"], b + 1)
                xs = x_all[:, span(b * T, T)]
                V.scalar_tensor_tensor(xs, HO[:, T:2 * T], c("outb"), xs, ALU.add, ALU.add).then_inc(S["xr_ready"], 1)

            def stats2(b, u):
                dve.wait_ge(S["xr_ready"], b + 1)
                own_wait(dve)
                V.bn_stats(st2[:, u % 2, :], x_all[:, span(b * T, T)]).then_inc(S["st2_done"], 1)

            def aggr2(b, u):
                dve.wait_ge(S["st2_done"], b + 1)
                wait(dve, S["r2_ready"], b - 1)
                own_wait(dve)
                V.bn_aggr(mv2[:, u % 2, :], st2[:, u % 2, :]).then_inc(S["mv2_ready"], 1)

            def normalise2(b, u):
                j = u % 2
                dve.wait_ge(S["r2_ready"], b + 1)
                wait(dve, S["hi_ready"], b - 1)
                V.tensor_scalar(xn2[:, j, :], x_all[:, span(b * T, T)], mv2[:, j, 0:1], r2[:, j:j + 1],
                                ALU.subtract, ALU.mult).then_inc(S["xn2_ready"], 1)

            def low(b, u):
                j = u % 2
                dve.wait_ge(S["hi_ready"], b + 1)
                V.tensor_tensor(rows_all[:, span(b * ROW + T, T)], xn2[:, j, :], rows_all[:, span(b * ROW, T)],
                                ALU.subtract).then_inc(S["lo_ready"], 1)

            def copy_xT(b, u):
                dve.wait_ge(S["xt_mm"], b + 1)
                V.tensor_copy(xT_all[:, span(b * 4 * P, 4 * P)], XB16).then_inc(S["xt_ready"], 1)

            def logits(b, u):
                dve.wait_ge(S["l_mm"], b + 1)
                V.tensor_scalar(lg[:, u * NE:(u + 1) * NE], LB[:, u * NE:(u + 1) * NE], 1 / WS, None, ALU.mult).then_inc(S["lg_ready"], 1)

            def weights_low(s, u):
                j = u % 2
                dve.wait_ge(S["wh_ready"], s + 1)
                V.scalar_tensor_tensor(w[:, span(s * WU + 2 * UP1, 2 * UP1)], wst13[:, j, :], WS,
                                       w[:, span(s * WU, 2 * UP1)], ALU.mult, ALU.subtract)
                V.scalar_tensor_tensor(w[0:FC, span(s * WU + W13 + 2 * T, 2 * T)], wst2[:, j, :], WS,
                                       w[0:FC, span(s * WU + W13, 2 * T)], ALU.mult, ALU.subtract).then_inc(S["wl_ready"], 1)

            def bc(a, n):
                return a.unsqueeze(2).broadcast_to([P, a.shape[1], n])

            def by_k(a):
                return rows3(a, NE).unsqueeze(2).broadcast_to([P, Q, TOPK, NE])

            def route_max(b0):
                dve.wait_ge(S["lg_ready"], b0 + 4)
                V.tensor_reduce(qm[:, :], rows3(lg, NE), AX.X, ALU.max).then_inc(S["route_max"], 4)

            def route_less_max(b0):
                dve.wait_ge(S["route_max"], b0 + 4)
                V.tensor_tensor(rows3(qz, NE), rows3(lg, NE), bc(qm[:, :], NE), ALU.subtract).then_inc(S["route_z"], 4)

            def route_sum(b0):
                dve.wait_ge(S["route_e"], b0 + 4)
                V.tensor_reduce(qs[:, :], rows3(qe, NE), AX.X, ALU.add).then_inc(S["route_sum"], 4)

            def route_recip(b0):
                dve.wait_ge(S["route_sum"], b0 + 4)
                V.reciprocal(qr[:, :], qs[:, :]).then_inc(S["route_recip"], 4)

            def route_score(b0):
                dve.wait_ge(S["route_recip"], b0 + 4)
                V.tensor_tensor(rows3(score, NE), rows3(qe, NE), bc(qr[:, :], NE), ALU.mult).then_inc(S["route_score"], 4)

            def group_max(b0):
                dve.wait_ge(S["route_score"], b0 + 4)
                V.tensor_reduce(gmax[:, :], rows3(score, NG), AX.X, ALU.max).then_inc(S["group_max"], 4)

            def group_compare(b0):
                gm = gmax[:, :].rearrange("p (q g) -> p q g", g=NG)
                other = gm.unsqueeze(2).broadcast_to([P, Q, NG, NG])
                own = gm.unsqueeze(3).broadcast_to([P, Q, NG, NG])
                dve.wait_ge(S["group_max"], b0 + 4)
                V.tensor_tensor(gcmp[:, :].rearrange("p (q g h) -> p q g h", g=NG, h=NG), other, own, ALU.is_gt)
                V.tensor_tensor(geq[:, :].rearrange("p (q g h) -> p q g h", g=NG, h=NG), other, own, ALU.is_equal).then_inc(S["group_cmp"], 4)

            def group_equal(b0):
                e3q = geq[:, :].rearrange("p (q g) -> p q g", q=Q)
                dve.wait_ge(S["group_cmp"], b0 + 4)
                V.tensor_tensor(e3q, e3q, c("lower").unsqueeze(1).broadcast_to([P, Q, NG * NG]), ALU.mult).then_inc(S["group_eq"], 4)

            def group_before(b0):
                dve.wait_ge(S["group_eq"], b0 + 4)
                V.tensor_tensor(gcmp[:, :], gcmp[:, :], geq[:, :], ALU.add).then_inc(S["group_before"], 4)

            def group_rank(b0):
                dve.wait_ge(S["group_before"], b0 + 4)
                V.tensor_reduce(grank[:, :], gcmp[:, :].rearrange("p (g h) -> p g h", h=NG), AX.X, ALU.add).then_inc(S["group_rank"], 4)

            def group_choose(b0):
                dve.wait_ge(S["group_rank"], b0 + 4)
                V.tensor_scalar(gsel[:, :], grank[:, :], float(TOPG), None, ALU.is_lt)
                V.tensor_scalar(gsub[:, :], grank[:, :], float(TOPG), -1.0, ALU.is_lt, ALU.add).then_inc(S["group_chosen"], 4)

            def mask_mult(b0):
                dve.wait_ge(S["group_chosen"], b0 + 4)
                V.tensor_tensor(rows3(masked, NG), rows3(score, NG), bc(gsel[:, :], NG), ALU.mult).then_inc(S["mask_mult"], 4)

            def mask_add(b0):
                dve.wait_ge(S["mask_mult"], b0 + 4)
                V.tensor_tensor(rows3(masked, NG), rows3(masked, NG), bc(gsub[:, :], NG), ALU.add).then_inc(S["masked"], 4)

            def top_values(b0):
                dve.wait_ge(S["masked"], b0 + 4)
                own_wait(dve)
                for q in range(Q):
                    i = V.max(top8[:, 8 * q:8 * q + 8], masked[:, q * NE:(q + 1) * NE])
                i.then_inc(S["top_values"], 4)

            def top_four(b0):
                dve.wait_ge(S["top_values"], b0 + 4)
                V.memset(rows3(top8, 8)[:, :, TOPK:8], -1.0).then_inc(S["top_four"], 4)

            def top_replace(b0):
                dve.wait_ge(S["top_four"], b0 + 4)
                own_wait(dve)
                for q in range(Q):
                    i = V.match_replace(repl[:, q * NE:(q + 1) * NE], top8[:, 8 * q:8 * q + 8], masked[:, q * NE:(q + 1) * NE], -2.0)
                i.then_inc(S["top_replaced"], 4)

            def chosen_diff(b0):
                dve.wait_ge(S["top_replaced"], b0 + 4)
                V.tensor_tensor(diff[:, :], masked[:, :], repl[:, :], ALU.subtract).then_inc(S["chosen_diff"], 4)

            def chosen(b0):
                dve.wait_ge(S["chosen_diff"], b0 + 4)
                V.tensor_scalar(sel16[:, :], diff[:, :], 2.0, None, ALU.is_ge).then_inc(S["sel_ready"], 4)
                V.tensor_scalar(sel[:, :], diff[:, :], 2.0, None, ALU.is_ge).then_inc(S["chosen"], 4)

            def rank_scan(b0):
                dve.wait_ge(S["chosen"], b0 + 4)
                V.tensor_tensor_scan(cum[:, :], c("carry"), sel[:, :], 0.0, ALU.mult, ALU.add).then_inc(S["rank_scan"], 4)

            def rank_mask(b0):
                dve.wait_ge(S["rank_scan"], b0 + 4)
                V.tensor_tensor(cum[:, :], cum[:, :], sel[:, :], ALU.mult).then_inc(S["rank"], 4)

            def rank_one_hot(b0):
                dve.wait_ge(S["rank"], b0 + 4)
                V.tensor_tensor(onek[:, :].rearrange("p (q k e) -> p q k e", q=Q, k=TOPK), by_k(cum),
                                c("rank").rearrange("p (k e) -> p k e", k=TOPK).unsqueeze(1).broadcast_to([P, Q, TOPK, NE]),
                                ALU.is_equal).then_inc(S["one_hot"], 4)

            def token_weights(b0):
                dve.wait_ge(S["chosen"], b0 + 4)
                V.tensor_tensor(rows3d[:, span(b0, Q), T:T + NE], rows3(score, NE), rows3(sel, NE), ALU.mult).then_inc(S["weights_set"], 4)

            def slots(b0):
                dve.wait_ge(S["pre_mm"], b0 + 4)
                V.tensor_tensor(rows3(slot, NE), LB[:, 64:64 + Q * NE].rearrange("p (q e) -> p q e", e=NE),
                                base[:, :].unsqueeze(1).broadcast_to([P, Q, NE]), ALU.add).then_inc(S["slots"], 4)
                dve.wait_ge(S["slots"], b0 + 4)
                V.tensor_tensor(base[:, :], base[:, :], LB[:, 128:128 + NE], ALU.add).then_inc(S["pre_read"], 4)

            def slots_by_rank(b0):
                dve.wait_ge(S["slots"], b0 + 4)
                dve.wait_ge(S["one_hot"], b0 + 4)
                V.tensor_tensor(onev[:, :].rearrange("p (q k e) -> p q k e", q=Q, k=TOPK),
                                onek[:, :].rearrange("p (q k e) -> p q k e", q=Q, k=TOPK), by_k(slot), ALU.mult).then_inc(S["slots_by_rank"], 4)

            def slots_sum(b0):
                dve.wait_ge(S["slots_by_rank"], b0 + 4)
                V.tensor_reduce(slot_f[:, span(b0 * TOPK, Q * TOPK)], onev[:, :].rearrange("p (q e) -> p q e", e=NE),
                                AX.X, ALU.add).then_inc(S["slots_sum"], 4)

            def slots_out(b0):
                dve.wait_ge(S["slots_sum"], b0 + 4)
                V.tensor_copy(slot_k[:, span(b0 * TOPK, Q * TOPK)], slot_f[:, span(b0 * TOPK, Q * TOPK)]).then_inc(S["slot_ready"], 4)

            def step(s, v):
                group(s, v, 8, token_weights)
                tile(s, v, 0, normalise)
                tile(s, v, 1, attended)
                group(s, v, 6, mask_add)
                tile(s, v, 2, aggr2)
                tile(s, v, 1, latent_stats)
                group(s, v, 6, top_values)
                tile(s, v, 1, latent_aggr)
                tile(s, v, 1, latent_moments)
                group(s, v, 6, top_four)
                tile(s, v, 2, normalise2)
                group(s, v, 6, top_replace)
                tile(s, v, 1, latent_all)
                tile(s, v, 1, latent_var)
                tile(s, v, 2, low)
                group(s, v, 6, chosen_diff)
                group(s, v, 6, chosen)
                group(s, v, 6, rank_scan)
                tile(s, v, 1, latent_centre)
                group(s, v, 8, slots_sum)
                tile(s, v, 1, latent_out)
                tile(s, v, 0, row_max)
                group(s, v, 6, rank_mask)
                tile(s, v, 2, copy_xT)
                group(s, v, 6, slots)
                tile(s, v, 0, weights_low, count=NU)
                tile(s, v, 2, logits)
                group(s, v, 5, route_max)
                group(s, v, 5, route_less_max)
                group(s, v, 5, route_sum)
                group(s, v, 8, slots_out)
                tile(s, v, 0, values)
                group(s, v, 5, route_recip)
                group(s, v, 5, route_score)
                group(s, v, 5, group_max)
                group(s, v, 6, rank_one_hot)
                group(s, v, 5, group_compare)
                tile(s, v, 1, residual)
                group(s, v, 7, slots_by_rank)
                group(s, v, 5, group_equal)
                tile(s, v, 0, recip)
                group(s, v, 5, group_before)
                group(s, v, 5, group_rank)
                group(s, v, 5, group_choose)
                tile(s, v, 1, stats2)
                group(s, v, 5, mask_mult)
            pipeline(dve, step)

            tv = [0]
            def link(i):
                tv[0] += 1
                i.then_inc(S["table_v"], 1)
                dve.wait_ge(S["table_v"], tv[0])
            dve.wait_ge(S["pre_read"], B)
            link(V.tensor_tensor(cnt[:, :], base[:, :], c("base"), ALU.subtract))
            V.tensor_copy(cnt_i[:, :], cnt[:, :]).then_inc(S["counts_ready"], 1)
            link(V.tensor_scalar(nt_a[:, :], cnt[:, :], float(P - 1), None, ALU.add))
            link(V.tensor_copy(nt_i[:, :], nt_a[:, :]))
            link(V.tensor_scalar(nt_s[:, :], nt_i[:, :], P.bit_length() - 1, None, ALU.logical_shift_right))
            link(V.tensor_copy(nt_f[:, :], nt_s[:, :]))
            link(V.memset(nt_a[:, :], 1.0))
            link(V.tensor_tensor_scan(ntc[:, :], nt_a[:, :], nt_f[:, :], 0.0, ALU.mult, ALU.add))
            i3 = ind.rearrange("p (t e) -> p t e", e=NE)
            c3 = indc.rearrange("p (t e) -> p t e", e=NE)
            ends = ntc[0:1, :].unsqueeze(1).broadcast_to([1, NT, NE])
            link(V.tensor_tensor(i3, ends, c("tau", 1).unsqueeze(2).broadcast_to([1, NT, NE]), ALU.is_le))
            link(V.tensor_reduce(te[:, :], i3, AX.X, ALU.add))
            link(V.tensor_tensor(c3, i3, ends, ALU.mult))
            link(V.tensor_reduce(tst0[:, :], c3, AX.X, ALU.max))
            link(V.tensor_tensor(trow[:, :], c("tau", 1), tst0[:, :], ALU.subtract))
            link(V.tensor_scalar(trow[:, :], trow[:, :], float(P), None, ALU.mult))
            link(V.tensor_scalar(tval[:, :], te[:, :], float(NE), None, ALU.is_lt))
            link(V.tensor_tensor(trow[:, :], trow[:, :], tval[:, :], ALU.mult))
            link(V.scalar_tensor_tensor(trow[:, :], te[:, :], float(REGION), trow[:, :], ALU.mult, ALU.add))
            link(V.tensor_tensor(te[:, :], te[:, :], tval[:, :], ALU.mult))
            link(V.tensor_copy(row_i[:, :], trow[:, :]))
            V.tensor_copy(exp_e[:, :], te[:, :])
            V.tensor_scalar(exp_i[:, :], te[:, :], float(WU), None, ALU.mult).then_inc(S["table_ready"], 1)

            def hidden(G, n, j):
                dve.wait_ge(G["silu_ready"], n + 1)
                V.scalar_tensor_tensor(hid[:, j, :], U[j][:, NF:UP1], 1 / WS, silu[:, j, :], ALU.mult, ALU.mult).then_inc(G["h_ready"], 1)

            def hidden_low(G, n, j, done, by):
                dve.wait_ge(G["hhi_ready"], n + 1)
                V.tensor_tensor(hh[:, j, NF:2 * NF], hid[:, j, :], hh[:, j, 0:NF], ALU.subtract).then_inc(done, by)

            def copy_hT(G, n, j, done, by):
                dve.wait_ge(G["ht_mm"], n + 1)
                wait(dve, G["dn_mm"], n - 1)
                V.tensor_copy(hT[:, j, :], H16[j]).then_inc(done, by)

            def sstep(b, u):
                n = 2 * b + u
                if shared(n, 0):
                    hidden(SH, n, u)
                if shared(n, 1):
                    copy_hT(SH, n - 1, 1 - u, SH["hT_ready"], 1)
                if shared(n, 0):
                    hidden_low(SH, n, u, SH["hlo_ready"], 1)
                if u == 1 and shared(n, 2):
                    dve.wait_ge(SH["dn_mm"], n - 1)
                    xs = x_all[:, span((b - 1) * T, T)]
                    V.scalar_tensor_tensor(xs, Y[0][:, 0:T], 1 / WS, xs, ALU.mult, ALU.add).then_inc(SH["y_ready"], 1)

            shared_pipeline(dve, sstep)

            def estep(s, v, r):
                v %= RING
                k = (v + 1) % 2
                if has(s, 3):
                    copy_hT(EX, s - 3, k, RS["hT_ready"][(v - 3) % RING], 16)
                if has(s, 1):
                    hidden(EX, s - 1, k)
                if has(s, 0):
                    dve.wait_ge(EX["xt_mm"], s + 1)
                    wait(dve, EX["up_mm"], s - 1)
                    V.tensor_copy(xT[:, v % 2, :], X16[v % 2])
                    V.tensor_copy(meta[:, span(s * META, META)], xg32[:, v, T:ROW32]).then_inc(RS["xt_ready"][v], 16)
                if has(s, 1):
                    hidden_low(EX, s - 1, k, RS["hlo_ready"][(v - 1) % RING], 16)

            expert_pipeline(dve, estep)

            CB = 4
            for n in range(B // CB):
                dve.wait_ge(part_in[n % 2], 32 * (n // 2 + 1))
                xs = x_all[:, CB * n * T:CB * (n + 1) * T]
                pj = [part[:, j, CB * (n % 2):CB * (n % 2) + CB, :].rearrange("p b t -> p (b t)") for j in range(2)]
                V.scalar_tensor_tensor(xs, pj[0], 1 / WS, xs, ALU.mult, ALU.add).then_inc(S["acc_v"], 1)
                dve.wait_ge(S["acc_v"], n + 1)
                V.scalar_tensor_tensor(xs, pj[1], 1 / WS, xs, ALU.mult, ALU.add).then_inc(acc_done, 1)

        @block.gpsimd
        def _(pool):
            G = nc.gpsimd
            pool.wait_ge(par_in, 32)
            pool.wait_ge(S["aggr_done"], B)
            G.tensor_scalar(r1[:, :], mv1[:, :, 1:2].rearrange("p b c -> p (b c)"), EPS, None, ALU.add).then_inc(S["r1_eps"], 1)
            pool.wait_ge(S["r1_eps"], 1)
            G.tensor_tensor(r1[:, :], r1[:, :], c("half"), ALU.pow).then_inc(S["r1_done"], 1)
            pool.wait_ge(ctx_in_s, 16)
            half = c("half")[:, 0:1]

            def add_context(b, u):
                pool.wait_ge(S["xn_ready"], b + 1)
                xs = x_all[:, b * T:(b + 1) * T]
                G.tensor_tensor(xs, xs, ctx_all[:, b * T:(b + 1) * T], ALU.add).then_inc(S["xc_ready"], 1)

            def latent_rstd(b, u):
                j = u % 2
                pool.wait_ge(S["vneg_ready"], b + 1)
                wait(pool, S["hpre_ready"], b - 1)
                G.tensor_scalar(vpos[:, j:j + 1], vneg[:, j:j + 1], -1.0, EPS, ALU.mult, ALU.add).then_inc(S["v_done"], 1)
                pool.wait_ge(S["v_done"], b + 1)
                G.tensor_tensor(trs[:, j:j + 1], vpos[:, j:j + 1], half, ALU.pow).then_inc(S["trs_ready"], 1)

            def rstd2(b, u):
                j = u % 2
                pool.wait_ge(S["mv2_ready"], b + 1)
                wait(pool, S["xn2_ready"], b - 1)
                G.tensor_scalar(v2[:, j:j + 1], mv2[:, j, 1:2], EPS, None, ALU.add).then_inc(S["v2_done"], 1)
                pool.wait_ge(S["v2_done"], b + 1)
                G.tensor_tensor(r2[:, j:j + 1], v2[:, j:j + 1], half, ALU.pow).then_inc(S["r2_ready"], 1)

            def scatter(b, u):
                if u == 0:
                    pool.wait_ge(S["slot_ready"], b + 4)
                    pool.wait_ge(S["weights_set"], b + 4)
                for k in range(TOPK):
                    G.indirect_dma_start(scatter_rows, bass.IndirectOffsetOnAxis(ap=slot_k[:, b * TOPK + k:b * TOPK + k + 1], axis=0),
                                         rows32[:, b * ROW32:(b + 1) * ROW32], None).then_inc(S["scattered"], 16)

            def step(s, v):
                tile(s, v, 3, rstd2)
                tile(s, v, 1, add_context)
                tile(s, v, 2, latent_rstd)
                tile(s, v, 10, scatter)
            for s in range(STEPS):
                step(s, s % 4)

            pool.wait_ge(S["sums_zero"], 32)

            def add_tile(t, j):
                pool.wait_ge(EX["y_ready"], t + 1)
                wait(pool, y_out[j], 8 * (t - j))
                G.tensor_copy(idx[:, j:j + 1], meta[:, span(t * META + NE, 1)]).then_inc(S["idx_set"], 1)
                pool.wait_ge(S["idx_set"], t + 1)
                own_wait(pool)
                G.indirect_dma_start(sums[j], bass.IndirectOffsetOnAxis(ap=idx[:, j:j + 1], axis=0),
                                     y_sb[:, j, :], None, compute_op=ALU.add).then_inc(y_out[j], 16)

            for t in range(2):
                add_tile(t, t)
            with pool.Fori(2, NT - 1, 2) as t:
                add_tile(t, 0)
                add_tile(t + 1, 1)


def constants():
    k = np.arange(P)
    tile = lambda a: np.broadcast_to(np.asarray(a, np.float32).reshape(1, -1), (P, np.asarray(a).size))
    g = np.arange(NG)
    return {
        "ident": np.eye(P, dtype=np.float32),
        "mean": np.full((P, P), 1.0 / P, np.float32),
        "lower": tile(g[None, :] < g[:, None]),
        "rank": tile(np.repeat(np.arange(1, TOPK + 1), NE)),
        "carry": tile(np.tile(np.arange(NE) > 0, 4)),
        "base": tile(np.arange(NE) * REGION),
        "token": (k[:, None] + P * np.arange(B)[None, :]).astype(np.float32),
        "pad": (TOKENS + k[:, None]).astype(np.float32),
        "tau": tile(np.arange(NT)),
        "half": np.full((P, NE), -0.5, np.float32),
    }, np.concatenate([np.eye(P), k[:, None] < k[None, :], np.ones((P, P))], 1).astype(np.float16)


def kernel(x, ctx_2048, L0_xattn_theta_w, L0_xattn_theta_b, L0_xattn_phi_w, L0_xattn_phi_b, L0_xattn_g_w,
           L0_xattn_g_b, L0_xattn_ln_gamma, L0_xattn_ln_beta, L0_xattn_out_w, L0_xattn_out_b, L0_ffn_Wg,
           L0_ffn_W1, L0_ffn_W3, L0_ffn_W2, L0_ffn_Ws1, L0_ffn_Ws3, L0_ffn_Ws2):
    import concourse.bacc as bacc
    from concourse.bass_utils import run_bass_kernel_spmd

    f = lambda a: np.asarray(a)
    consts, halves = constants()

    def rows(a):
        full = np.zeros((P, a.shape[1]), np.float32)
        full[:a.shape[0]] = a
        return full

    latent = lambda a: f(a).T.reshape(2, P, L).transpose(1, 0, 2).reshape(P, 2 * L)
    consts.update({
        "gamma": latent(L0_xattn_ln_gamma), "beta": latent(L0_xattn_ln_beta),
        "gb": np.broadcast_to(np.tile(f(L0_xattn_g_b), 2), (P, 2 * L)),
        "thw": f(L0_xattn_theta_w).T, "phw": f(L0_xattn_phi_w).T, "gw": f(L0_xattn_g_w).T,
        "wg": f(L0_ffn_Wg).T.reshape(2, P, NE).transpose(1, 0, 2).reshape(P, 2 * NE),
        "outw": rows(f(L0_xattn_out_w).T), "outb": f(L0_xattn_out_b).reshape(P, 1),
        "thb": rows(f(L0_xattn_theta_b).reshape(L, 1)), "phb": rows(f(L0_xattn_phi_b).reshape(L, 1)),
    })
    params = np.concatenate([consts[n] for n in COLS], 1)
    assert params.shape == (P, NCOLS)

    w1 = np.concatenate([f(L0_ffn_W1), f(L0_ffn_Ws1).reshape(2, NF, T)])
    w3 = np.concatenate([f(L0_ffn_W3), f(L0_ffn_Ws3).reshape(2, NF, T)])
    w2 = np.concatenate([f(L0_ffn_W2), f(L0_ffn_Ws2).reshape(T, 2, NF).transpose(1, 0, 2)])
    w13 = np.concatenate([w1, w3], 1).transpose(0, 2, 1).reshape(NU, 2, P, UP1).transpose(0, 2, 1, 3).reshape(NU, P, 2 * UP1)
    w2 = w2.transpose(0, 2, 1).reshape(NU, 2, FC, T).transpose(0, 2, 1, 3).reshape(NU, FC, 2 * T)

    arrays = {"x_dram": f(x), "ctx_dram": f(ctx_2048), "params_dram": params, "halves_dram": halves,
              "w13_dram": w13, "w2_dram": w2}
    arrays = {n: np.ascontiguousarray(a) for n, a in arrays.items()}
    nc = bacc.Bacc("TRN2", target_bir_lowering=False, num_devices=1)
    args = [nc.dram_tensor(n, a.shape, mybir.dt.from_np(a.dtype), kind="ExternalInput").ap() for n, a in arrays.items()]
    out = nc.dram_tensor("out_dram", (B, P, T), F32, kind="ExternalOutput").ap()
    build(nc, *args, out)
    r = run_bass_kernel_spmd(nc, [arrays], core_ids=[0])
    return r.results[0]["out_dram"]
```

```python
from contextlib import ExitStack

import numpy as np

import concourse.bass as bass
from concourse import mybir

ALU = mybir.AluOpType
ACT = mybir.ActivationFunctionType
AX = mybir.AxisListType
F32 = mybir.dt.float32
F16 = mybir.dt.float16
I32 = mybir.dt.int32
U32 = mybir.dt.uint32

P = 128
B = 16
T = 256
L = 64
NE = 16
NU = NE + 2
NF = 176
FC = NF // 2
NG = 4
TOPG = 2
TOPK = 4
EPS = 1e-5
WS = 64.0
REGION = B * P + P
NT = (B * P * TOPK + NE * (P - 1)) // P + 1
NT += -NT % 8
SLOTS = NE * REGION
UP1 = 2 * NF
W13 = 2 * 2 * UP1
W2 = 2 * 2 * T
WU = W13 + W2
ROW32 = T + NE + 1
ROW = 2 * ROW32
TOKENS = B * P

COLS = {}
_at = 0
for _n, _w in (("ident", P), ("mean", P), ("lower", NG * NG), ("rank", TOPK * NE), ("carry", 4 * NE),
               ("base", NE), ("token", B), ("pad", 1), ("tau", NT), ("half", NE), ("gamma", 2 * L), ("beta", 2 * L), ("gb", 2 * L),
               ("thw", L), ("phw", L), ("gw", L), ("wg", 2 * NE), ("outw", P), ("thb", 1), ("phb", 1)):
    COLS[_n] = (_at, _at + _w)
    _at += _w
NCOLS = _at
SMALL = COLS["outw"][1] - COLS["thw"][0]


def build(nc, x, ctx_in, params, halves, w13_in, w2_in, out):
    scatter_rows = nc.dram_tensor("slot_rows", (SLOTS + P, ROW32), F32, kind="Internal").ap()
    sums = [nc.dram_tensor(f"sums{j}", (TOKENS + P, T), F32, kind="Internal").ap() for j in range(2)]

    with ExitStack() as stack:
        def sb(name, shape, dt=F32):
            return stack.enter_context(nc.sbuf_tensor(name, shape, dt))

        def sem(name):
            return stack.enter_context(nc.semaphore(name))

        def span(at, n):
            return slice(at, at + n) if isinstance(at, int) else bass.ds(at, n)

        def wait(eng, s, n):
            if not isinstance(n, int) or n > 0:
                eng.wait_ge(s, n)

        def own_wait(eng):
            eng.nop(nofuse=True)

        par = sb("par", [P, NCOLS])
        hal = sb("hal", [P, 3 * P], F16)
        ident16, tri16, ones16 = hal[:, 0:P], hal[:, P:2 * P], hal[:, 2 * P:3 * P]

        def c(name, rows=P):
            a, b = COLS[name]
            return par[0:rows, a:b]

        small_at = COLS["thw"][0]

        def small(name, part, rows=P):
            a, b = COLS[name]
            return small16[0:rows, part, a - small_at:b - small_at]

        x_all = sb("x_all", [P, B * T])
        ctx_all = sb("ctx_all", [P, B * T])
        rows32 = sb("rows_all", [P, B * ROW32])
        rows_all = rows32[:, :].bitcast(F16)
        xT_all = sb("xT_all", [P, B * 4 * P], F16)
        w = sb("w", [P, NU * WU], F16)
        wst13 = sb("wst13", [P, 2, 2 * UP1])
        wst2 = sb("wst2", [FC, 2, 2 * T])
        small16 = sb("small16", [P, 2, SMALL], F16)
        xn16 = sb("xn16", [P, 2, 2, T], F16)
        ctx16 = sb("ctx16", [P, 2, 2, T], F16)
        st1 = sb("st1", [P, B, 6])
        mv1 = sb("mv1", [P, B, 2])
        r1 = sb("r1", [P, B])
        xn = sb("xn", [P, 2, T])
        th = sb("th", [L, 2, T])
        ph = sb("ph", [L, 2, T])
        g_sb = sb("g_sb", [P, 2, 2 * L])
        nmax = sb("nmax", [P, 2, 2])
        psums = sb("psums", [P, 2, 2])
        rsum = sb("rsum", [P, 2, 2])
        p_sb = sb("p_sb", [P, 2, 2 * T])
        pT = sb("pT", [P, 2, 2 * T])
        tx = sb("tx", [P, 2, 2 * L])
        tst = sb("tst", [P, 2, 6])
        tmv = sb("tmv", [P, 2, 2])
        gmv = sb("gmv", [P, 2, 2])
        vneg = sb("vneg", [P, 2])
        vpos = sb("vpos", [P, 2])
        trs = sb("trs", [P, 2])
        hpre = sb("hpre", [P, 2, 2 * L])
        hr16 = sb("hr16", [L + 1, 2, 2, T], F16)
        st2 = sb("st2", [P, 2, 6])
        mv2 = sb("mv2", [P, 2, 2])
        v2 = sb("v2", [P, 2])
        r2 = sb("r2", [P, 2])
        xn2 = sb("xn2", [P, 2, T])
        Q = 4
        lg = sb("lg", [P, Q * NE])
        qm = sb("qm", [P, Q])
        qs = sb("qs", [P, Q])
        qr = sb("qr", [P, Q])
        qz = sb("qz", [P, Q * NE])
        qe = sb("qe", [P, Q * NE])
        score = sb("score", [P, Q * NE])
        gmax = sb("gmax", [P, Q * NG])
        gcmp = sb("gcmp", [P, Q * NG * NG])
        geq = sb("geq", [P, Q * NG * NG])
        grank = sb("grank", [P, Q * NG])
        gsel = sb("gsel", [P, Q * NG])
        gsub = sb("gsub", [P, Q * NG])
        masked = sb("masked", [P, Q * NE])
        top8 = sb("top8", [P, Q * 8])
        repl = sb("repl", [P, Q * NE])
        sel = sb("sel", [P, Q * NE])
        diff = sb("diff", [P, Q * NE])
        sel16 = sb("sel16", [P, Q * NE], F16)
        cum = sb("cum", [P, Q * NE])
        base = sb("base", [P, NE])
        pad_rows = sb("pad_rows", [P, ROW32])
        slot = sb("slot", [P, Q * NE])
        onek = sb("onek", [P, Q * TOPK * NE])
        slot_f = sb("slot_f", [P, B * TOPK])
        slot_k = sb("slot_k", [P, B * TOPK], U32)
        cnt = sb("cnt", [P, NE])
        cnt_i = sb("cnt_i", [P, NE], I32)
        nt_a = sb("nt_a", [P, NE])
        nt_i = sb("nt_i", [P, NE], I32)
        nt_s = sb("nt_s", [P, NE], I32)
        nt_f = sb("nt_f", [P, NE])
        ntc = sb("ntc", [P, NE])
        row_i = sb("row_i", [1, NT], I32)
        exp_e = sb("exp_e", [1, NT], I32)
        exp_i = sb("exp_i", [1, NT], I32)
        silu = sb("silu", [P, 2, NF])
        hid = sb("hid", [P, 2, NF])
        hh = sb("hh", [P, 2, 2 * NF], F16)
        hT = sb("hT", [FC, 2, 4 * P], F16)
        m = NT * NE
        ind, indc = ctx_all[0:1, 0:m], ctx_all[0:1, m:2 * m]
        te, tst0, trow, tval = (ctx_all[0:1, 2 * m + n * NT:2 * m + (n + 1) * NT] for n in range(4))
        RING = 4
        META = NE + 1
        _at = [0]

        def reuse(n):
            _at[0] += n
            assert _at[0] <= B * T
            return ctx_all[:, _at[0] - n:_at[0]]

        meta = reuse(NT * META)
        xg32 = reuse(RING * ROW32)
        xg = xg32.bitcast(F16).rearrange("p (j c) -> p j c", j=RING)
        xg32 = xg32.rearrange("p (j c) -> p j c", j=RING)
        xT = reuse(2 * 2 * P).bitcast(F16).rearrange("p (j c) -> p j c", j=2)
        y_sb = reuse(2 * T).rearrange("p (j c) -> p j c", j=2)
        CB = 4

        def part(n, j):
            at = ((n % 2) * 2 + j) * 2 * CB * T
            return (xT_all if n < 2 else w)[:, at:at + 2 * CB * T].bitcast(F32)

        idx = sb("idx", [P, 2], U32)

        bank = [stack.enter_context(nc.psum_tensor(f"bank{i}", [P, 512], F32)) for i in range(8)]
        TP, GP, SP_, PT, TS, HO, XB, LB = [b[:, :] for b in bank]
        XB16 = XB.bitcast(F16)[:, 0:4 * P]

        ctx_in_s = [sem("ctx_in0"), sem("ctx_in1")]
        par_in, wst_in0, wst_in1 = sem("par_in"), sem("wst_in0"), sem("wst_in1")
        x_in = [sem(f"x_in{i}") for i in range(4)]
        wst_in = [wst_in0, wst_in1]
        names = ("stat_done aggr_done r1_eps r1_done small_hi small_lo base_set xn_ready xhi_ready xlo_ready "
                 "chi_ready clo_ready hrlo_ready xc_ready th_mm ph_mm thph_ready g_mm g_ready s_mm max_ready "
                 "p_ready pt_mm pt_ready rs_ready t_mm tx_ready ts_done ta_done tmv_ready st_mm gmv_done vneg_ready "
                 "v_done trs_ready hc_done hpre_ready ht_mm hr_ready o_mm xr_ready st2_done mv2_ready v2_done "
                 "r2_ready xn2_ready hi_ready lo_ready xt_mm xt_ready l_mm lg_ready wh_ready wl_ready "
                 "route_max route_z route_e route_sum route_recip route_score group_max group_cmp group_eq group_before "
                 "group_rank group_chosen mask_mult masked top_values top_four top_replaced chosen_diff chosen rank_scan "
                 "rank one_hot weights_set slots slots_by_rank slots_sum sel_ready pre_mm pre_read "
                 "slot_ready scattered zero_set counts_ready "
                 "table_v table_ready tails_in out_written acc_v sums_zero meta_set idx_set").split()
        S = {n: sem(n) for n in names}
        part_in = [sem(f"part_in{n}") for n in range(B // CB)]
        acc_done = sem("acc_done")

        FFN = "xt_mm xt_ready up_mm silu_ready h_ready hhi_ready hlo_ready ht_mm hT_ready dn_mm y_ready".split()
        SH = {n: sem(f"sh_{n}") for n in FFN}
        EX = {n: sem(f"ex_{n}") for n in FFN}

        LAG = {"xg_in": 0, "xt_ready": 1, "hlo_ready": 3, "hT_ready": 3}
        RS = {n: [sem(f"ex_{n}{m}") for m in range(RING)] for n in LAG}

        def ring_count(name, t, rel=None):
            if isinstance(t, int):
                return 16 * (t // RING + 1) + (16 if t % RING >= RING - LAG[name] else 0)
            m = rel % RING
            return 4 * (t - m) + 16 + (16 if m >= RING - LAG[name] else 0)

        y_out = [sem("y_out0"), sem("y_out1")]

        FIRST = 8
        STEPS = B + 5
        S_LOOP = 12
        POOL_LAG = 13
        AFTER_COUNT = 6

        R1_WAITS = {0: 1, 4: 2, 7: 4}

        def pipeline(eng, step, shared_step, between=None):
            between = between or (lambda stage, n: None)
            for s in range(FIRST):
                step(s, s % 4)
                between("A", s)
            with eng.Fori(FIRST, B - 3, 4) as i:
                for v in range(4):
                    step(i + v, v)
            for s in range(B, STEPS):
                step(s, s % 4)
            for b in range(S_LOOP):
                for u in range(2):
                    shared_step(b, u)
                    between("S", 2 * b + u)
            with eng.Fori(S_LOOP, B) as b:
                for u in range(2):
                    shared_step(b, u)
            for u in range(2):
                shared_step(B, u)

        def tile(s, v, lag, part, count=B):
            if not isinstance(s, int) or 0 <= s - lag < count:
                part(s - lag, (v - lag) % 4)

        def group(s, v, lag, part):
            if (v - lag) % 4 == 0 and (not isinstance(s, int) or 0 <= s - lag < B - 4):
                part(s - lag)

        BODY = 6 * RING
        assert (NT - 2 * RING) % BODY == 0

        def expert_pipeline(eng, step, lags=3):
            for s in range(2 * RING):
                step(s, s % RING, None)
            with eng.Fori(2 * RING, NT - BODY + 1, BODY) as i:
                for v in range(BODY):
                    if v % RING == 0:
                        r = eng.snap(4 * (i + v) + 16)
                    step(i + v, v, r)
            for s in range(NT, NT + lags):
                step(s, s % RING, None)

        def has(s, lag):
            return not isinstance(s, int) or 0 <= s - lag < NT

        def shared(n, lag):
            return not isinstance(n, int) or 0 <= n - lag < 2 * B

        U, H, Y = [TP, GP], [SP_, PT], [TS, HO]
        X16 = [b.bitcast(F16)[:, 0:4 * P] for b in (XB, LB)]
        H16 = [h.bitcast(F16)[0:FC, 0:4 * P] for h in H]

        block = stack.enter_context(nc.Block())

        @block.sync
        def _(sp):
            xv = x.rearrange("b p t -> p b t")
            cv = ctx_in.rearrange("b p t -> p b t")
            x3 = x_all[:, :].rearrange("p (b t) -> p b t", t=T)
            c3 = ctx_all[:, :].rearrange("p (b t) -> p b t", t=T)
            sp.dma_start(x3[:, 0:4, :], xv[:, 0:4, :]).then_inc(x_in[0], 16)
            sp.dma_start(par[:, :], params).then_inc(par_in, 16)
            sp.dma_start(c3[:, 0:4, :], cv[:, 0:4, :]).then_inc(ctx_in_s[0], 16)
            sp.dma_start(hal[:, :], halves).then_inc(par_in, 16)
            for n in range(1, 4):
                sp.dma_start(x3[:, 4 * n:4 * n + 4, :], xv[:, 4 * n:4 * n + 4, :]).then_inc(x_in[n], 16)
                if n == 1:
                    sp.dma_start(c3[:, 4:B, :], cv[:, 4:B, :]).then_inc(ctx_in_s[1], 16)

            def load_weights(e, j):
                wait(sp, S["wl_ready"], e - 1)
                sp.dma_start(wst13[:, j, :], w13_in[span(e, 1), :, :].rearrange("a p f -> (a p) f")).then_inc(wst_in[j], 16)
                sp.dma_start(wst2[:, j, :], w2_in[span(e, 1), :, :].rearrange("a p f -> (a p) f")).then_inc(wst_in[j], 16)

            for e in range(2):
                load_weights(e, e)
            with sp.Fori(2, NU - 1, 2) as e:
                load_weights(e, 0)
                load_weights(e + 1, 1)

            sp.wait_ge(S["zero_set"], 1)
            for j in range(2):
                sp.dma_start(sums[j].rearrange("(b p) t -> p b t", p=P),
                             pad_rows[:, 0:T].unsqueeze(1).broadcast_to([P, B + 1, T])).then_inc(S["sums_zero"], 16)

            sp.dma_start(scatter_rows[SLOTS:SLOTS + P, :], pad_rows[:, :]).then_inc(S["tails_in"], 16)
            sp.wait_ge(S["counts_ready"], 1)
            with sp.Fori(0, NE) as e:
                n = sp.value_load(cnt_i[0:1, span(e, 1)], min_val=0, max_val=TOKENS)
                sp.dma_start(scatter_rows[bass.ds(e * REGION + n, P), :], pad_rows[:, :]).then_inc(S["tails_in"], 16)

            sp.wait_ge(S["tails_in"], 16 * (NE + 1))
            sp.wait_ge(S["scattered"], 16 * B * TOPK)
            sp.wait_ge(S["table_ready"], 1)

            def load_tile(t, v):
                if not isinstance(t, int) or t >= RING:
                    sp.wait_ge(RS["xt_ready"][v], ring_count("xt_ready", t - RING, v))
                r = sp.value_load(row_i[0:1, span(t, 1)], min_val=0, max_val=SLOTS)
                sp.dma_start(xg32[:, v, :], scatter_rows[bass.ds(r, P), :]).then_inc(RS["xg_in"][v], 16)

            for t in range(RING):
                load_tile(t, t)
            with sp.Fori(RING, NT - RING + 1, RING) as t:
                for v in range(RING):
                    load_tile(t + v, v)

            for j in range(2):
                sp.wait_ge(y_out[j], 8 * NT)
            sv = [a[0:TOKENS, :].rearrange("(b p) t -> p b t", p=P) for a in sums]
            ov = out.rearrange("b p t -> p b t")
            for n in range(B // CB):
                for j in range(2):
                    sp.dma_start(part(n, j).rearrange("p (b t) -> p b t", t=T), sv[j][:, CB * n:CB * n + CB, :]).then_inc(part_in[n], 16)
            for n in range(B // CB):
                sp.wait_ge(acc_done, n + 1)
                sp.dma_start(ov[:, CB * n:CB * n + CB, :],
                             x_all[:, CB * n * T:CB * (n + 1) * T].rearrange("p (b t) -> p b t", t=T)).then_inc(S["out_written"], 16)
            sp.wait_ge(S["out_written"], 16 * B // CB)

        @block.scalar
        def _(act):
            A = nc.scalar.activation
            act.wait_ge(par_in, 32)

            def weights_high(s, u):
                j = u % 2
                act.wait_ge(wst_in[j], 16 * s + 32 - 16 * j)
                A(w[:, span(s * WU, 2 * UP1)], wst13[:, j, :], ACT.Copy, scale=WS)
                A(w[0:FC, span(s * WU + W13, 2 * T)], wst2[:, j, :], ACT.Copy, scale=WS).then_inc(S["wh_ready"], 1)

            def theta_phi(b, u):
                j = u % 2
                act.wait_ge(S["th_mm"], b + 1)
                act.wait_ge(S["ph_mm"], b + 1)
                wait(act, S["s_mm"], b - 1)
                A(th[:, j, :], TP[0:L, 0:T], ACT.Identity, bias=c("thb", L), scale=1 / WS)
                A(ph[:, j, :], TP[0:L, T:2 * T], ACT.Identity, bias=c("phb", L), scale=1 / WS).then_inc(S["thph_ready"], 1)

            def exps(b, u):
                j = u % 2
                act.wait_ge(S["max_ready"], b + 1)
                wait(act, S["pt_mm"], b - 1)
                wait(act, S["rs_ready"], b - 1)
                for h in range(2):
                    i = A(p_sb[:, j, h * T:(h + 1) * T], SP_[:, h * T:(h + 1) * T], ACT.Exp,
                          bias=nmax[:, j, h:h + 1], accum_out=psums[:, j, h:h + 1])
                i.then_inc(S["p_ready"], 1)

            def copy_pT(b, u):
                j = u % 2
                act.wait_ge(S["pt_mm"], b + 1)
                wait(act, S["t_mm"], b - 1)
                A(pT[:, j, :], PT, ACT.Copy).then_inc(S["pt_ready"], 1)

            def relu(b, u):
                j = u % 2
                act.wait_ge(S["ht_mm"], b + 1)
                wait(act, S["o_mm"], b - 1)
                A(hr16[0:L, j, 0, :], HO[0:L, 0:T], ACT.Relu).then_inc(S["hr_ready"], 1)

            def high(b, u):
                j = u % 2
                act.wait_ge(S["xn2_ready"], b + 1)
                A(rows_all[:, span(b * ROW, T)], xn2[:, j, :], ACT.Copy).then_inc(S["hi_ready"], 1)

            def normalised_high(b, u):
                act.wait_ge(S["xn_ready"], b + 1)
                wait(act, S["g_mm"], b - 1)
                wait(act, S["ph_mm"], b - 1)
                A(xn16[:, u % 2, 0, :], xn[:, u % 2, :], ACT.Copy).then_inc(S["xhi_ready"], 1)

            def context_high(b, u):
                if isinstance(b, int) and b in (0, 4):
                    act.wait_ge(ctx_in_s[b // 4], 16)
                wait(act, S["th_mm"], b - 1)
                A(ctx16[:, u % 2, 0, :], ctx_all[:, span(b * T, T)], ACT.Copy).then_inc(S["chi_ready"], 1)

            def copy_xT(b, u):
                act.wait_ge(S["xt_mm"], b + 1)
                A(xT_all[:, span(b * 4 * P, 4 * P)], XB16, ACT.Copy).then_inc(S["xt_ready"], 1)

            def route_exp(b0):
                act.wait_ge(S["route_z"], b0 + 4)
                A(qe[:, :], qz[:, :], ACT.Exp).then_inc(S["route_e"], 4)

            def step(s, v):
                tile(s, v, 2, exps)
                tile(s, v, 0, context_high)
                tile(s, v, 5, copy_xT)
                tile(s, v, 1, theta_phi)
                tile(s, v, 2, copy_pT)
                tile(s, v, 3, relu)
                tile(s, v, 4, high)
                tile(s, v, 0, normalised_high)
                tile(s, v, 2, weights_high, count=NU)
                group(s, v, 8, route_exp)

            def gate(G, n, j):
                act.wait_ge(G["up_mm"], n + 1)
                A(silu[:, j, :], U[j][:, 0:NF], ACT.Silu, scale=1 / WS).then_inc(G["silu_ready"], 1)

            def hidden_high(G, n, j):
                act.wait_ge(G["h_ready"], n + 1)
                wait(act, G["ht_mm"], n - 1)
                A(hh[:, j, 0:NF], hid[:, j, :], ACT.Copy).then_inc(G["hhi_ready"], 1)

            def sstep(b, u):
                n = 2 * b + u
                if shared(n, 0):
                    gate(SH, n, u)
                if shared(n, 1):
                    act.wait_ge(SH["ht_mm"], n)
                    wait(act, SH["dn_mm"], n - 2)
                    A(hT[:, 1 - u, :], H16[1 - u], ACT.Copy).then_inc(SH["hT_ready"], 1)
                if shared(n, 0):
                    hidden_high(SH, n, u)

            def between(stage, n):
                if stage == "S" and n == 0:
                    route_exp(B - Q)

            pipeline(act, step, sstep, between)

            def estep(s, v, r):
                v %= RING
                k = (v + 1) % 2
                if has(s, 1):
                    gate(EX, s - 1, k)
                if has(s, 1):
                    hidden_high(EX, s - 1, k)
                if has(s, 3):
                    t = s - 3
                    e = act.value_load(exp_e[0:1, span(t, 1)], min_val=0, max_val=NE - 1)
                    act.wait_ge(EX["dn_mm"], t + 1)
                    wait(act, y_out[k], 8 * (t - k))
                    A(y_sb[:, k, :], Y[k][:, 0:T], ACT.Copy, scale=meta[:, span(t * META + e, 1)]).then_inc(EX["y_ready"], 1)

            expert_pipeline(act, estep)

        @block.tensor
        def _(pe):
            mm, tr = nc.tensor.matmul, nc.tensor.transpose
            ident = c("ident")
            pe.wait_ge(par_in, 32)
            pe.wait_ge(S["small_lo"], 1)

            def wparts(to, name, of, rows=P):
                for n, (wpart, part) in enumerate(((0, 0), (0, 1), (1, 0))):
                    i = mm(to, small(name, wpart, rows), of[:, part, :], start=n == 0, stop=n == 2)
                return i

            def theta(b, u):
                pe.wait_ge(S["clo_ready"], b + 1)
                wait(pe, S["thph_ready"], b)
                wparts(TP[0:L, 0:T], "thw", ctx16[:, u % 2, :, :]).then_inc(S["th_mm"], 1)

            def phi(b, u):
                pe.wait_ge(S["xlo_ready"], b + 1)
                wparts(TP[0:L, T:2 * T], "phw", xn16[:, u % 2, :, :]).then_inc(S["ph_mm"], 1)

            def project_g(b, u):
                pe.wait_ge(S["xlo_ready"], b + 1)
                wait(pe, S["g_ready"], b)
                for h in range(2):
                    for n, (wpart, part) in enumerate(((0, 0), (0, 1), (1, 0))):
                        i = mm(GP[:, h * L:(h + 1) * L], xn16[:, u % 2, part, h * P:(h + 1) * P], small("gw", wpart),
                               start=n == 0, stop=n == 2)
                i.then_inc(S["g_mm"], 1)

            def scores(b, u):
                j = u % 2
                pe.wait_ge(S["thph_ready"], b + 1)
                wait(pe, S["p_ready"], b)
                for h in range(2):
                    i = mm(SP_[:, h * T:(h + 1) * T], th[:, j, h * P:(h + 1) * P], ph[:, j, :], start=True, stop=True)
                i.then_inc(S["s_mm"], 1)

            def transpose_p(b, u):
                j = u % 2
                pe.wait_ge(S["p_ready"], b + 1)
                wait(pe, S["pt_ready"], b)
                for h in range(2):
                    for k in range(2):
                        i = tr(PT[:, k * T + h * P:k * T + h * P + P], p_sb[:, j, h * T + k * P:h * T + k * P + P], ident)
                i.then_inc(S["pt_mm"], 1)

            def attend(b, u):
                j = u % 2
                pe.wait_ge(S["pt_ready"], b + 1)
                pe.wait_ge(S["g_ready"], b + 1)
                wait(pe, S["gmv_done"], b)
                for h in range(2):
                    for k in range(2):
                        i = mm(TS[:, h * L:(h + 1) * L], pT[:, j, k * T + h * P:k * T + h * P + P],
                               g_sb[:, j, k * L:(k + 1) * L], start=k == 0, stop=k == 1)
                i.then_inc(S["t_mm"], 1)

            def mean_all(b, u):
                j = u % 2
                pe.wait_ge(S["tmv_ready"], b + 1)
                mm(TS[:, 2 * L:2 * L + 2], c("mean"), tmv[:, j, :], start=True, stop=True).then_inc(S["st_mm"], 1)

            def transpose_h(b, u):
                j = u % 2
                pe.wait_ge(S["hpre_ready"], b + 1)
                wait(pe, S["xr_ready"], b)
                own_wait(pe)
                for h in range(2):
                    i = tr(HO[0:L, h * P:(h + 1) * P], hpre[:, j, h * L:(h + 1) * L], ident)
                i.then_inc(S["ht_mm"], 1)

            def project_out(b, u):
                j = u % 2
                pe.wait_ge(S["hrlo_ready"], b + 1)
                wparts(HO[:, T:2 * T], "outw", hr16[:, j, :, :], L + 1).then_inc(S["o_mm"], 1)

            def transpose_rows(b, u):
                pe.wait_ge(S["lo_ready"], b + 1)
                wait(pe, S["xt_ready"], b)
                for k in range(4):
                    i = tr(XB16[:, k * P:(k + 1) * P], rows_all[:, span(b * ROW + k * P, P)], ident16)
                i.then_inc(S["xt_mm"], 1)

            def router(b, u):
                pe.wait_ge(S["xt_ready"], b + 1)
                wait(pe, S["lg_ready"], b)
                if u == AFTER_COUNT % 4 and (not isinstance(b, int) or b >= AFTER_COUNT):
                    pe.wait_ge(S["pre_read"], b - AFTER_COUNT + 4)
                for k in range(4):
                    for w in range(2):
                        i = mm(LB[:, u * NE:(u + 1) * NE], xT_all[:, span((b * 4 + k) * P, P)],
                               small("wg", w)[:, (k % 2) * NE:(k % 2 + 1) * NE], start=k == 0 and w == 0, stop=k == 3 and w == 1)
                i.then_inc(S["l_mm"], 1)

            def count(b0):
                pe.wait_ge(S["sel_ready"], b0 + 4)
                pe.wait_ge(S["lg_ready"], min(b0 + AFTER_COUNT, B) if isinstance(b0, int) else b0 + AFTER_COUNT)
                for u in range(4):
                    for v in range(u + 1):
                        mm(LB[:, 64 + u * NE:64 + (u + 1) * NE], tri16 if v == u else ones16,
                           sel16[:, v * NE:(v + 1) * NE], start=v == 0, stop=v == u)
                for v in range(4):
                    i = mm(LB[:, 128:128 + NE], ones16, sel16[:, v * NE:(v + 1) * NE], start=v == 0, stop=v == 3)
                i.then_inc(S["pre_mm"], 4)

            def step(s, v):
                tile(s, v, 2, scores)
                tile(s, v, 4, project_out)
                tile(s, v, 3, mean_all)
                tile(s, v, 1, theta)
                tile(s, v, 5, transpose_rows)
                tile(s, v, 1, phi)
                group(s, v, 11, count)
                tile(s, v, 2, transpose_p)
                tile(s, v, 1, project_g)
                tile(s, v, 5, router)
                tile(s, v, 3, transpose_h)
                tile(s, v, 2, attend)

            def up(done, j, xt, wcol):
                for k in range(2):
                    for wpart, part in ((0, 0), (0, 1), (1, 0)):
                        i = mm(U[j][:, 0:UP1], xt(2 * part + k), w[:, span(wcol + (2 * wpart + k) * UP1, UP1)],
                               start=k == 0 and (wpart, part) == (0, 0), stop=k == 1 and wpart == 1)
                i.then_inc(done, 1)

            def transpose_hidden(done, j):
                for k in range(4):
                    i = tr(H16[j][:, k * P:(k + 1) * P], hh[:, j, k * FC:(k + 1) * FC], ident16)
                i.then_inc(done, 1)

            def down(done, j, y, wcol, start, stop):
                for k in range(2):
                    for wpart, part in ((0, 0), (0, 1), (1, 0)):
                        i = mm(y[:, 0:T], hT[:, j, (2 * part + k) * P:(2 * part + k + 1) * P],
                               w[0:FC, span(wcol + W13 + (2 * wpart + k) * T, T)],
                               start=start and k == 0 and (wpart, part) == (0, 0), stop=stop and k == 1 and wpart == 1)
                i.then_inc(done, 1)

            def sstep(b, u):
                n = 2 * b + u
                if isinstance(b, int) and b < 2:
                    if n == 0:
                        pe.wait_ge(S["wl_ready"], 2)
                    for name in (("thph_ready",), ("g_ready", "p_ready"), ("pt_ready", "gmv_done"), ())[n]:
                        pe.wait_ge(S[name], B)
                if shared(n, 0):
                    wait(pe, SH["h_ready"], n - 1)
                    up(SH["up_mm"], u, lambda k: xT_all[:, span((b * 4 + k) * P, P)], u * WU)
                if shared(n, 1):
                    pe.wait_ge(SH["hlo_ready"], n)
                    wait(pe, SH["hT_ready"], n - 2)
                    transpose_hidden(SH["ht_mm"], 1 - u)
                if shared(n, 2):
                    if u == 0:
                        wait(pe, SH["y_ready"], b - 1)
                    pe.wait_ge(SH["hT_ready"], n - 1)
                    down(SH["dn_mm"], u, Y[0], u * WU, start=u == 0, stop=u == 1)

            def between(stage, n):
                if stage == "S" and n == 8:
                    count(B - Q)

            pipeline(pe, step, sstep, between)

            pe.wait_ge(S["table_ready"], 1)
            pe.wait_ge(S["wl_ready"], NU)
            pe.wait_ge(SH["y_ready"], B)
            for name in ("xr_ready", "xt_ready", "pre_read"):
                pe.wait_ge(S[name], B)

            up_weights = {}

            def estep(s, step_v, r):
                v = step_v % RING
                k = (v + 1) % 2

                def ready(name, lag):
                    t = s - lag
                    pe.wait_ge(RS[name][(v - lag) % RING], ring_count(name, t) if r is None else r)

                if has(s, 3):
                    ready("hlo_ready", 3)
                    transpose_hidden(EX["ht_mm"], k)
                if has(s, 0):
                    ready("xg_in", 0)
                    for q in range(4):
                        i = tr(X16[v % 2][:, q * P:(q + 1) * P], xg[:, v, q * P:(q + 1) * P], ident16)
                    i.then_inc(EX["xt_mm"], 1)
                if has(s, 1):
                    e = pe.value_load(exp_i[0:1, span(s - 1, 1)], min_val=2 * WU, max_val=(NU - 1) * WU)
                    up_weights[step_v] = e
                    ready("xt_ready", 1)
                    up(EX["up_mm"], k, lambda q: xT[:, k, q * P:(q + 1) * P], e)
                if has(s, 3):
                    if r is not None and step_v >= 2:
                        e = up_weights[step_v - 2]
                    else:
                        e = pe.value_load(exp_i[0:1, span(s - 3, 1)], min_val=2 * WU, max_val=(NU - 1) * WU)
                    ready("hT_ready", 3)
                    if r is None and s >= NT:
                        pe.wait_ge(EX["y_ready"], s - 4)
                    down(EX["dn_mm"], k, Y[k], e, start=True, stop=True)

            expert_pipeline(pe, estep)

        @block.vector
        def _(dve):
            V = nc.vector
            rows3d = rows32[:, :].rearrange("p (b c) -> p b c", c=ROW32)
            rows3 = lambda a, n: a[:, :].rearrange("p (q e) -> p q e", e=n)

            def stats1(n):
                dve.wait_ge(x_in[n], 16)
                for b in range(4 * n, 4 * n + 4):
                    V.bn_stats(st1[:, b, :], x_all[:, b * T:(b + 1) * T]).then_inc(S["stat_done"], 1)
                for b in range(4 * n, 4 * n + 4):
                    dve.wait_ge(S["stat_done"], b + 1)
                    V.bn_aggr(mv1[:, b, :], st1[:, b, :]).then_inc(S["aggr_done"], 1)

            V.memset(pad_rows[:, :], 0.0).then_inc(S["meta_set"], 1)
            V.memset(hr16[L:L + 1, :, 0, :], 1.0)
            V.memset(hr16[L:L + 1, :, 1, :], 0.0)
            stats1(0)
            dve.wait_ge(par_in, 32)
            for name, lag in LAG.items():
                for m in range(RING - lag, RING):
                    dve.sem_inc(RS[name][m], 16)
            V.tensor_copy(rows3d[:, :, ROW32 - 1:ROW32], c("token").unsqueeze(2))
            dve.wait_ge(S["meta_set"], 1)
            V.tensor_copy(pad_rows[:, ROW32 - 1:ROW32], c("pad")).then_inc(S["zero_set"], 1)
            small32 = par[:, small_at:small_at + SMALL]
            V.tensor_scalar(small16[:, 0, :], small32, WS, None, ALU.mult).then_inc(S["small_hi"], 1)
            V.tensor_copy(base[:, :], c("base")).then_inc(S["base_set"], 1)
            dve.wait_ge(S["small_hi"], 1)
            V.scalar_tensor_tensor(small16[:, 1, :], small32, WS, small16[:, 0, :], ALU.mult, ALU.subtract).then_inc(S["small_lo"], 1)

            def normalise(b, u):
                j = u % 2
                if isinstance(b, int) and b in R1_WAITS:
                    dve.wait_ge(S["r1_done"], R1_WAITS[b])
                wait(dve, S["xlo_ready"], b - 1)
                V.tensor_scalar(xn[:, j, :], x_all[:, span(b * T, T)], mv1[:, span(b, 1), 0:1].rearrange("p a c -> p (a c)"),
                                r1[:, span(b, 1)], ALU.subtract, ALU.mult).then_inc(S["xn_ready"], 1)

            def relu_low(b, u):
                dve.wait_ge(S["hr_ready"], b + 1)
                V.scalar_tensor_tensor(hr16[0:L, u % 2, 1, :], HO[0:L, 0:T], 0.0, hr16[0:L, u % 2, 0, :], ALU.max, ALU.subtract).then_inc(S["hrlo_ready"], 1)

            def values(b, u):
                j = u % 2
                dve.wait_ge(S["g_mm"], b + 1)
                wait(dve, S["t_mm"], b - 1)
                V.scalar_tensor_tensor(g_sb[:, j, :], GP[:, 0:2 * L], 1 / WS, c("gb"), ALU.mult, ALU.add).then_inc(S["g_ready"], 1)

            def row_max(b, u):
                j = u % 2
                dve.wait_ge(S["s_mm"], b + 1)
                wait(dve, S["p_ready"], b - 1)
                V.tensor_reduce(nmax[:, j, :], SP_.rearrange("p (h t) -> p h t", h=2), AX.X, ALU.max, negate=True).then_inc(S["max_ready"], 1)

            def recip(b, u):
                j = u % 2
                dve.wait_ge(S["p_ready"], b + 1)
                V.reciprocal(rsum[:, j, :], psums[:, j, :]).then_inc(S["rs_ready"], 1)

            def attended(b, u):
                j = u % 2
                dve.wait_ge(S["rs_ready"], b + 1)
                dve.wait_ge(S["t_mm"], b + 1)
                V.tensor_tensor(tx[:, j, :].rearrange("p (h l) -> p h l", h=2), TS[:, 0:2 * L].rearrange("p (h l) -> p h l", h=2),
                                rsum[:, j, :].unsqueeze(2).broadcast_to([P, 2, L]), ALU.mult).then_inc(S["tx_ready"], 1)

            def latent_stats(b, u):
                dve.wait_ge(S["tx_ready"], b + 1)
                own_wait(dve)
                V.bn_stats(tst[:, u % 2, :], tx[:, u % 2, :]).then_inc(S["ts_done"], 1)

            def latent_aggr(b, u):
                dve.wait_ge(S["ts_done"], b + 1)
                own_wait(dve)
                V.bn_aggr(tmv[:, u % 2, :], tst[:, u % 2, :]).then_inc(S["ta_done"], 1)

            def latent_moments(b, u):
                j = u % 2
                dve.wait_ge(S["ta_done"], b + 1)
                V.scalar_tensor_tensor(tmv[:, j, 1:2], tmv[:, j, 0:1], tmv[:, j, 0:1], tmv[:, j, 1:2], ALU.mult, ALU.add).then_inc(S["tmv_ready"], 1)

            def latent_all(b, u):
                dve.wait_ge(S["st_mm"], b + 1)
                V.tensor_copy(gmv[:, u % 2, :], TS[:, 2 * L:2 * L + 2]).then_inc(S["gmv_done"], 1)

            def latent_var(b, u):
                j = u % 2
                dve.wait_ge(S["gmv_done"], b + 1)
                wait(dve, S["trs_ready"], b - 1)
                V.scalar_tensor_tensor(vneg[:, j:j + 1], gmv[:, j, 0:1], gmv[:, j, 0:1], gmv[:, j, 1:2],
                                       ALU.mult, ALU.subtract).then_inc(S["vneg_ready"], 1)

            def latent_centre(b, u):
                j = u % 2
                V.scalar_tensor_tensor(tx[:, j, :], tx[:, j, :], gmv[:, j, 0:1], c("gamma"), ALU.subtract, ALU.mult).then_inc(S["hc_done"], 1)

            def latent_out(b, u):
                j = u % 2
                dve.wait_ge(S["hc_done"], b + 1)
                dve.wait_ge(S["trs_ready"], b + 1)
                wait(dve, S["ht_mm"], b - 1)
                V.scalar_tensor_tensor(hpre[:, j, :], tx[:, j, :], trs[:, j:j + 1], c("beta"), ALU.mult, ALU.add).then_inc(S["hpre_ready"], 1)

            def residual(b, u):
                dve.wait_ge(S["o_mm"], b + 1)
                dve.wait_ge(S["xc_ready"], b + 1)
                xs = x_all[:, span(b * T, T)]
                V.scalar_tensor_tensor(xs, HO[:, T:2 * T], 1 / WS, xs, ALU.mult, ALU.add).then_inc(S["xr_ready"], 1)

            def stats2(b, u):
                dve.wait_ge(S["xr_ready"], b + 1)
                own_wait(dve)
                V.bn_stats(st2[:, u % 2, :], x_all[:, span(b * T, T)]).then_inc(S["st2_done"], 1)

            def aggr2(b, u):
                dve.wait_ge(S["st2_done"], b + 1)
                wait(dve, S["r2_ready"], b - 1)
                own_wait(dve)
                V.bn_aggr(mv2[:, u % 2, :], st2[:, u % 2, :]).then_inc(S["mv2_ready"], 1)

            def normalise2(b, u):
                j = u % 2
                dve.wait_ge(S["r2_ready"], b + 1)
                wait(dve, S["lo_ready"], b - 1)
                V.tensor_scalar(xn2[:, j, :], x_all[:, span(b * T, T)], mv2[:, j, 0:1], r2[:, j:j + 1],
                                ALU.subtract, ALU.mult).then_inc(S["xn2_ready"], 1)

            def logits(b, u):
                dve.wait_ge(S["l_mm"], b + 1)
                V.tensor_scalar(lg[:, u * NE:(u + 1) * NE], LB[:, u * NE:(u + 1) * NE], 1 / WS, None, ALU.mult).then_inc(S["lg_ready"], 1)

            def weights_low(s, u):
                j = u % 2
                dve.wait_ge(S["wh_ready"], s + 1)
                V.scalar_tensor_tensor(w[:, span(s * WU + 2 * UP1, 2 * UP1)], wst13[:, j, :], WS,
                                       w[:, span(s * WU, 2 * UP1)], ALU.mult, ALU.subtract)
                V.scalar_tensor_tensor(w[0:FC, span(s * WU + W13 + 2 * T, 2 * T)], wst2[:, j, :], WS,
                                       w[0:FC, span(s * WU + W13, 2 * T)], ALU.mult, ALU.subtract).then_inc(S["wl_ready"], 1)

            def bc(a, n):
                return a.unsqueeze(2).broadcast_to([P, a.shape[1], n])

            def by_k(a):
                return rows3(a, NE).unsqueeze(2).broadcast_to([P, Q, TOPK, NE])

            def route_max(b0):
                dve.wait_ge(S["lg_ready"], b0 + 4)
                V.tensor_reduce(qm[:, :], rows3(lg, NE), AX.X, ALU.max).then_inc(S["route_max"], 4)

            def route_less_max(b0):
                dve.wait_ge(S["route_max"], b0 + 4)
                V.tensor_tensor(rows3(qz, NE), rows3(lg, NE), bc(qm[:, :], NE), ALU.subtract).then_inc(S["route_z"], 4)

            def route_sum(b0):
                dve.wait_ge(S["route_e"], b0 + 4)
                V.tensor_reduce(qs[:, :], rows3(qe, NE), AX.X, ALU.add).then_inc(S["route_sum"], 4)

            def route_recip(b0):
                dve.wait_ge(S["route_sum"], b0 + 4)
                V.reciprocal(qr[:, :], qs[:, :]).then_inc(S["route_recip"], 4)

            def route_score(b0):
                dve.wait_ge(S["route_recip"], b0 + 4)
                V.tensor_tensor(rows3(score, NE), rows3(qe, NE), bc(qr[:, :], NE), ALU.mult).then_inc(S["route_score"], 4)

            def group_max(b0):
                dve.wait_ge(S["route_score"], b0 + 4)
                V.tensor_reduce(gmax[:, :], rows3(score, NG), AX.X, ALU.max).then_inc(S["group_max"], 4)

            def group_compare(b0):
                gm = gmax[:, :].rearrange("p (q g) -> p q g", g=NG)
                other = gm.unsqueeze(2).broadcast_to([P, Q, NG, NG])
                own = gm.unsqueeze(3).broadcast_to([P, Q, NG, NG])
                dve.wait_ge(S["group_max"], b0 + 4)
                V.tensor_tensor(gcmp[:, :].rearrange("p (q g h) -> p q g h", g=NG, h=NG), other, own, ALU.is_gt)
                V.tensor_tensor(geq[:, :].rearrange("p (q g h) -> p q g h", g=NG, h=NG), other, own, ALU.is_equal).then_inc(S["group_cmp"], 4)

            def group_equal(b0):
                e3q = geq[:, :].rearrange("p (q g) -> p q g", q=Q)
                dve.wait_ge(S["group_cmp"], b0 + 4)
                V.tensor_tensor(e3q, e3q, c("lower").unsqueeze(1).broadcast_to([P, Q, NG * NG]), ALU.mult).then_inc(S["group_eq"], 4)

            def group_before(b0):
                dve.wait_ge(S["group_eq"], b0 + 4)
                V.tensor_tensor(gcmp[:, :], gcmp[:, :], geq[:, :], ALU.add).then_inc(S["group_before"], 4)

            def group_rank(b0):
                dve.wait_ge(S["group_before"], b0 + 4)
                V.tensor_reduce(grank[:, :], gcmp[:, :].rearrange("p (g h) -> p g h", h=NG), AX.X, ALU.add).then_inc(S["group_rank"], 4)

            def group_choose(b0):
                dve.wait_ge(S["group_rank"], b0 + 4)
                V.tensor_scalar(gsel[:, :], grank[:, :], float(TOPG), None, ALU.is_lt)
                V.tensor_scalar(gsub[:, :], grank[:, :], float(TOPG), -1.0, ALU.is_lt, ALU.add).then_inc(S["group_chosen"], 4)

            def mask_mult(b0):
                dve.wait_ge(S["group_chosen"], b0 + 4)
                V.tensor_tensor(rows3(masked, NG), rows3(score, NG), bc(gsel[:, :], NG), ALU.mult).then_inc(S["mask_mult"], 4)

            def mask_add(b0):
                dve.wait_ge(S["mask_mult"], b0 + 4)
                V.tensor_tensor(rows3(masked, NG), rows3(masked, NG), bc(gsub[:, :], NG), ALU.add).then_inc(S["masked"], 4)

            def top_values(b0):
                dve.wait_ge(S["masked"], b0 + 4)
                own_wait(dve)
                for q in range(Q):
                    i = V.max(top8[:, 8 * q:8 * q + 8], masked[:, q * NE:(q + 1) * NE])
                i.then_inc(S["top_values"], 4)

            def top_four(b0):
                dve.wait_ge(S["top_values"], b0 + 4)
                V.memset(rows3(top8, 8)[:, :, TOPK:8], -1.0).then_inc(S["top_four"], 4)

            def top_replace(b0):
                dve.wait_ge(S["top_four"], b0 + 4)
                own_wait(dve)
                for q in range(Q):
                    i = V.match_replace(repl[:, q * NE:(q + 1) * NE], top8[:, 8 * q:8 * q + 8], masked[:, q * NE:(q + 1) * NE], -2.0)
                i.then_inc(S["top_replaced"], 4)

            def chosen_diff(b0):
                dve.wait_ge(S["top_replaced"], b0 + 4)
                V.tensor_tensor(diff[:, :], masked[:, :], repl[:, :], ALU.subtract).then_inc(S["chosen_diff"], 4)

            def chosen(b0):
                dve.wait_ge(S["chosen_diff"], b0 + 4)
                V.tensor_scalar(sel16[:, :], diff[:, :], 2.0, None, ALU.is_ge).then_inc(S["sel_ready"], 4)
                V.tensor_scalar(sel[:, :], diff[:, :], 2.0, None, ALU.is_ge).then_inc(S["chosen"], 4)

            def rank_scan(b0):
                dve.wait_ge(S["chosen"], b0 + 4)
                V.tensor_tensor_scan(cum[:, :], c("carry"), sel[:, :], 0.0, ALU.mult, ALU.add).then_inc(S["rank_scan"], 4)

            def rank_mask(b0):
                dve.wait_ge(S["rank_scan"], b0 + 4)
                V.tensor_tensor(cum[:, :], cum[:, :], sel[:, :], ALU.mult).then_inc(S["rank"], 4)

            def rank_one_hot(b0):
                dve.wait_ge(S["rank"], b0 + 4)
                V.tensor_tensor(onek[:, :].rearrange("p (q k e) -> p q k e", q=Q, k=TOPK), by_k(cum),
                                c("rank").rearrange("p (k e) -> p k e", k=TOPK).unsqueeze(1).broadcast_to([P, Q, TOPK, NE]),
                                ALU.is_equal).then_inc(S["one_hot"], 4)

            def token_weights(b0):
                dve.wait_ge(S["chosen"], b0 + 4)
                V.tensor_tensor(rows3d[:, span(b0, Q), T:T + NE], rows3(score, NE), rows3(sel, NE), ALU.mult).then_inc(S["weights_set"], 4)

            def slots(b0):
                dve.wait_ge(S["pre_mm"], b0 + 4)
                V.tensor_tensor(rows3(slot, NE), LB[:, 64:64 + Q * NE].rearrange("p (q e) -> p q e", e=NE),
                                base[:, :].unsqueeze(1).broadcast_to([P, Q, NE]), ALU.add).then_inc(S["slots"], 4)
                dve.wait_ge(S["slots"], b0 + 4)
                V.tensor_tensor(base[:, :], base[:, :], LB[:, 128:128 + NE], ALU.add).then_inc(S["pre_read"], 4)

            def slots_by_rank(b0):
                dve.wait_ge(S["slots"], b0 + 4)
                dve.wait_ge(S["one_hot"], b0 + 4)
                V.tensor_tensor(onek[:, :].rearrange("p (q k e) -> p q k e", q=Q, k=TOPK),
                                onek[:, :].rearrange("p (q k e) -> p q k e", q=Q, k=TOPK), by_k(slot), ALU.mult).then_inc(S["slots_by_rank"], 4)

            def slots_sum(b0):
                dve.wait_ge(S["slots_by_rank"], b0 + 4)
                V.tensor_reduce(slot_f[:, span(b0 * TOPK, Q * TOPK)], onek[:, :].rearrange("p (q e) -> p q e", e=NE),
                                AX.X, ALU.add).then_inc(S["slots_sum"], 4)

            def slots_out(b0):
                dve.wait_ge(S["slots_sum"], b0 + 4)
                V.tensor_copy(slot_k[:, span(b0 * TOPK, Q * TOPK)], slot_f[:, span(b0 * TOPK, Q * TOPK)]).then_inc(S["slot_ready"], 4)

            def step(s, v):
                tile(s, v, 3, attended)
                tile(s, v, 3, latent_stats)
                tile(s, v, 3, latent_aggr)
                tile(s, v, 3, latent_moments)
                group(s, v, 10, mask_mult)
                group(s, v, 11, chosen_diff)
                group(s, v, 9, route_sum)
                tile(s, v, 2, row_max)
                group(s, v, 11, chosen)
                group(s, v, 9, route_recip)
                group(s, v, 11, rank_scan)
                tile(s, v, 4, residual)
                group(s, v, 10, mask_add)
                group(s, v, 11, rank_mask)
                group(s, v, 9, route_score)
                tile(s, v, 3, latent_all)
                tile(s, v, 2, values)
                tile(s, v, 3, latent_var)
                tile(s, v, 4, stats2)
                group(s, v, 9, group_max)
                tile(s, v, 3, latent_centre)
                tile(s, v, 4, aggr2)
                group(s, v, 11, rank_one_hot)
                group(s, v, 11, slots)
                group(s, v, 9, group_compare)
                tile(s, v, 0, normalise)
                group(s, v, 10, top_values)
                tile(s, v, 3, latent_out)
                group(s, v, 9, group_equal)
                tile(s, v, 3, weights_low, count=NU)
                tile(s, v, 4, normalise2)
                group(s, v, 11, slots_by_rank)
                group(s, v, 10, top_four)
                tile(s, v, 5, logits)
                tile(s, v, 2, recip)
                group(s, v, 9, group_before)
                group(s, v, 11, token_weights)
                group(s, v, 11, slots_sum)
                group(s, v, 9, group_rank)
                tile(s, v, 3, relu_low)
                group(s, v, 11, slots_out)
                group(s, v, 8, route_max)
                group(s, v, 9, group_choose)
                group(s, v, 8, route_less_max)
                group(s, v, 10, top_replace)

            def hidden(G, n, j):
                dve.wait_ge(G["silu_ready"], n + 1)
                V.scalar_tensor_tensor(hid[:, j, :], U[j][:, NF:UP1], 1 / WS, silu[:, j, :], ALU.mult, ALU.mult).then_inc(G["h_ready"], 1)

            def hidden_low(G, n, j, done, by):
                dve.wait_ge(G["hhi_ready"], n + 1)
                V.tensor_tensor(hh[:, j, NF:2 * NF], hid[:, j, :], hh[:, j, 0:NF], ALU.subtract).then_inc(done, by)

            tv = [0]
            def link(i):
                tv[0] += 1
                i.then_inc(S["table_v"], 1)
                dve.wait_ge(S["table_v"], tv[0])
            i3 = ind.rearrange("p (t e) -> p t e", e=NE)
            c3 = indc.rearrange("p (t e) -> p t e", e=NE)
            ends = ntc[0:1, :].unsqueeze(1).broadcast_to([1, NT, NE])

            def count_tokens():
                dve.wait_ge(S["pre_read"], B)
                link(V.tensor_tensor(cnt[:, :], base[:, :], c("base"), ALU.subtract))
                V.tensor_copy(cnt_i[:, :], cnt[:, :]).then_inc(S["counts_ready"], 1)
                link(V.tensor_scalar(nt_a[:, :], cnt[:, :], float(P - 1), None, ALU.add))
                link(V.tensor_copy(nt_i[:, :], nt_a[:, :]))

            def count_tiles():
                link(V.tensor_scalar(nt_s[:, :], nt_i[:, :], P.bit_length() - 1, None, ALU.logical_shift_right))
                link(V.tensor_copy(nt_f[:, :], nt_s[:, :]))
                link(V.memset(nt_a[:, :], 1.0))
                link(V.tensor_tensor_scan(ntc[:, :], nt_a[:, :], nt_f[:, :], 0.0, ALU.mult, ALU.add))

            def experts_before():
                link(V.tensor_tensor(i3, ends, c("tau", 1).unsqueeze(2).broadcast_to([1, NT, NE]), ALU.is_le))

            def tile_expert():
                link(V.tensor_reduce(te[:, :], i3, AX.X, ALU.add))

            def tiles_before():
                link(V.tensor_tensor(c3, i3, ends, ALU.mult))

            def row_in_expert():
                link(V.tensor_reduce(tst0[:, :], c3, AX.X, ALU.max))
                link(V.tensor_tensor(trow[:, :], c("tau", 1), tst0[:, :], ALU.subtract))
                link(V.tensor_scalar(trow[:, :], trow[:, :], float(P), None, ALU.mult))

            def tile_used():
                link(V.tensor_scalar(tval[:, :], te[:, :], float(NE), None, ALU.is_lt))
                link(V.tensor_tensor(trow[:, :], trow[:, :], tval[:, :], ALU.mult))
                link(V.scalar_tensor_tensor(trow[:, :], te[:, :], float(REGION), trow[:, :], ALU.mult, ALU.add))

            def tile_row():
                link(V.tensor_tensor(te[:, :], te[:, :], tval[:, :], ALU.mult))
                link(V.tensor_copy(row_i[:, :], trow[:, :]))

            def tile_weights():
                V.tensor_copy(exp_e[:, :], te[:, :])
                V.tensor_scalar(exp_i[:, :], te[:, :], float(WU), float(2 * WU), ALU.mult, ALU.add).then_inc(S["table_ready"], 1)

            b0 = B - Q

            def between(stage, n):
                if stage == "A":
                    if n < 3:
                        stats1(n + 1)
                elif n == 0:
                    route_max(b0)
                    route_less_max(b0)
                elif n == 1:
                    route_sum(b0)
                    route_recip(b0)
                elif n == 2:
                    route_score(b0)
                    group_max(b0)
                elif n == 3:
                    group_compare(b0)
                    group_equal(b0)
                elif n == 4:
                    group_before(b0)
                    group_rank(b0)
                elif n == 5:
                    group_choose(b0)
                    mask_mult(b0)
                elif n == 6:
                    mask_add(b0)
                    top_values(b0)
                elif n == 7:
                    top_four(b0)
                    top_replace(b0)
                elif n == 8:
                    chosen_diff(b0)
                    chosen(b0)
                elif n == 9:
                    rank_scan(b0)
                    rank_mask(b0)
                elif n == 10:
                    token_weights(b0)
                    slots(b0)
                elif n == 11:
                    rank_one_hot(b0)
                elif n == 12:
                    slots_by_rank(b0)
                elif n == 13:
                    slots_sum(b0)
                    slots_out(b0)
                elif n == 14:
                    count_tokens()
                elif n == 15:
                    count_tiles()
                elif n == 16:
                    experts_before()
                elif n == 17:
                    tile_expert()
                elif n == 18:
                    tiles_before()
                elif n == 19:
                    row_in_expert()
                elif n == 20:
                    tile_used()
                elif n == 21:
                    tile_row()
                elif n == 22:
                    tile_weights()

            def sstep(b, u):
                n = 2 * b + u
                if shared(n, 0):
                    hidden(SH, n, u)
                if isinstance(b, int):
                    between("S", n)
                if shared(n, 0):
                    hidden_low(SH, n, u, SH["hlo_ready"], 1)
                if u == 1 and shared(n, 2):
                    dve.wait_ge(SH["dn_mm"], n - 1)
                    xs = x_all[:, span((b - 1) * T, T)]
                    V.scalar_tensor_tensor(xs, Y[0][:, 0:T], 1 / WS, xs, ALU.mult, ALU.add).then_inc(SH["y_ready"], 1)

            pipeline(dve, step, sstep, lambda stage, n: stage == "A" and between(stage, n))

            def estep(s, v, r):
                v %= RING
                k = (v + 1) % 2
                if has(s, 3):
                    dve.wait_ge(EX["ht_mm"], s - 2)
                    wait(dve, EX["dn_mm"], s - 4)
                    V.tensor_copy(hT[:, k, :], H16[k]).then_inc(RS["hT_ready"][(v - 3) % RING], 16)
                if has(s, 0):
                    dve.wait_ge(EX["xt_mm"], s + 1)
                    wait(dve, EX["up_mm"], s - 1)
                    V.tensor_copy(meta[:, span(s * META, META)], xg32[:, v, T:ROW32])
                    V.tensor_copy(xT[:, v % 2, :], X16[v % 2]).then_inc(RS["xt_ready"][v], 16)
                if has(s, 2):
                    hidden_low(EX, s - 2, v % 2, RS["hlo_ready"][(v - 2) % RING], 16)
                if has(s, 1):
                    hidden(EX, s - 1, k)

            expert_pipeline(dve, estep)

            for n in range(B // CB):
                dve.wait_ge(part_in[n], 32)
                xs = x_all[:, CB * n * T:CB * (n + 1) * T]
                V.scalar_tensor_tensor(xs, part(n, 0), 1 / WS, xs, ALU.mult, ALU.add).then_inc(S["acc_v"], 1)
                dve.wait_ge(S["acc_v"], n + 1)
                V.scalar_tensor_tensor(xs, part(n, 1), 1 / WS, xs, ALU.mult, ALU.add).then_inc(acc_done, 1)

        @block.gpsimd
        def _(pool):
            G = nc.gpsimd
            pool.wait_ge(par_in, 32)

            def rstd1(n):
                rs = r1[:, 4 * n:4 * n + 4]
                pool.wait_ge(S["aggr_done"], 4 * n + 4)
                G.tensor_scalar(rs, mv1[:, 4 * n:4 * n + 4, 1:2].rearrange("p b c -> p (b c)"), EPS, None, ALU.add).then_inc(S["r1_eps"], 1)
                pool.wait_ge(S["r1_eps"], n + 1)
                G.tensor_tensor(rs, rs, c("half")[:, 0:4], ALU.pow).then_inc(S["r1_done"], 1)

            rstd1(0)
            half = c("half")[:, 0:1]

            def add_context(b, u):
                pool.wait_ge(S["xn_ready"], b + 1)
                if b in (0, 4):
                    pool.wait_ge(ctx_in_s[b // 4], 16)
                xs = x_all[:, b * T:(b + 1) * T]
                G.tensor_tensor(xs, xs, ctx_all[:, b * T:(b + 1) * T], ALU.add).then_inc(S["xc_ready"], 1)

            def context_low(b, u):
                pool.wait_ge(S["chi_ready"], b + 1)
                G.tensor_tensor(ctx16[:, u % 2, 1, :], ctx_all[:, b * T:(b + 1) * T], ctx16[:, u % 2, 0, :], ALU.subtract).then_inc(S["clo_ready"], 1)

            def latent_rstd(b, u):
                j = u % 2
                pool.wait_ge(S["vneg_ready"], b + 1)
                wait(pool, S["hpre_ready"], b - 1)
                G.tensor_scalar(vpos[:, j:j + 1], vneg[:, j:j + 1], -1.0, EPS, ALU.mult, ALU.add).then_inc(S["v_done"], 1)
                pool.wait_ge(S["v_done"], b + 1)
                G.tensor_tensor(trs[:, j:j + 1], vpos[:, j:j + 1], half, ALU.pow).then_inc(S["trs_ready"], 1)

            def rstd2(b, u):
                j = u % 2
                pool.wait_ge(S["mv2_ready"], b + 1)
                wait(pool, S["xn2_ready"], b - 1)
                G.tensor_scalar(v2[:, j:j + 1], mv2[:, j, 1:2], EPS, None, ALU.add).then_inc(S["v2_done"], 1)
                pool.wait_ge(S["v2_done"], b + 1)
                G.tensor_tensor(r2[:, j:j + 1], v2[:, j:j + 1], half, ALU.pow).then_inc(S["r2_ready"], 1)

            def normalised_low(b, u):
                pool.wait_ge(S["xhi_ready"], b + 1)
                G.tensor_tensor(xn16[:, u % 2, 1, :], xn[:, u % 2, :], xn16[:, u % 2, 0, :], ALU.subtract).then_inc(S["xlo_ready"], 1)

            def low(b, u):
                pool.wait_ge(S["hi_ready"], b + 1)
                G.tensor_tensor(rows_all[:, b * ROW + T:b * ROW + 2 * T], xn2[:, u % 2, :], rows_all[:, b * ROW:b * ROW + T],
                                ALU.subtract).then_inc(S["lo_ready"], 1)

            def scatter_to(k):
                def part(b, u):
                    if u == 0:
                        pool.wait_ge(S["slot_ready"], b + 4)
                        pool.wait_ge(S["weights_set"], b + 4)
                    G.indirect_dma_start(scatter_rows, bass.IndirectOffsetOnAxis(ap=slot_k[:, b * TOPK + k:b * TOPK + k + 1], axis=0),
                                         rows32[:, b * ROW32:(b + 1) * ROW32], None).then_inc(S["scattered"], 16)
                return part

            scatter = [scatter_to(k) for k in range(TOPK)]

            def step(s, v):
                tile(s, v, 5, low)
                tile(s, v, 1, context_low)
                tile(s, v, 1, normalised_low)
                tile(s, v, 13, scatter[0])
                tile(s, v, 12, scatter[3])
                tile(s, v, 3, latent_rstd)
                tile(s, v, 2, add_context)
                tile(s, v, 4, rstd2)
                tile(s, v, 12, scatter[1])
                tile(s, v, 13, scatter[2])
            for s in range(B + POOL_LAG):
                step(s, s % 4)
                if 1 <= s <= 3:
                    rstd1(s)

            pool.wait_ge(S["sums_zero"], 32)

            def add_tile(t, j):
                pool.wait_ge(EX["y_ready"], t + 1)
                wait(pool, y_out[j], 8 * (t - j))
                G.tensor_copy(idx[:, j:j + 1], meta[:, span(t * META + NE, 1)]).then_inc(S["idx_set"], 1)
                pool.wait_ge(S["idx_set"], t + 1)
                own_wait(pool)
                G.indirect_dma_start(sums[j], bass.IndirectOffsetOnAxis(ap=idx[:, j:j + 1], axis=0),
                                     y_sb[:, j, :], None, compute_op=ALU.add).then_inc(y_out[j], 16)

            for t in range(2):
                add_tile(t, t)
            with pool.Fori(2, NT - 1, 2) as t:
                add_tile(t, 0)
                add_tile(t + 1, 1)


def constants():
    k = np.arange(P)
    tile = lambda a: np.broadcast_to(np.asarray(a, np.float32).reshape(1, -1), (P, np.asarray(a).size))
    g = np.arange(NG)
    return {
        "ident": np.eye(P, dtype=np.float32),
        "mean": np.full((P, P), 1.0 / P, np.float32),
        "lower": tile(g[None, :] < g[:, None]),
        "rank": tile(np.repeat(np.arange(1, TOPK + 1), NE)),
        "carry": tile(np.tile(np.arange(NE) > 0, 4)),
        "base": tile(np.arange(NE) * REGION),
        "token": (k[:, None] + P * np.arange(B)[None, :]).astype(np.float32),
        "pad": (TOKENS + k[:, None]).astype(np.float32),
        "tau": tile(np.arange(NT)),
        "half": np.full((P, NE), -0.5, np.float32),
    }, np.concatenate([np.eye(P), k[:, None] < k[None, :], np.ones((P, P))], 1).astype(np.float16)


def kernel(x, ctx_2048, L0_xattn_theta_w, L0_xattn_theta_b, L0_xattn_phi_w, L0_xattn_phi_b, L0_xattn_g_w,
           L0_xattn_g_b, L0_xattn_ln_gamma, L0_xattn_ln_beta, L0_xattn_out_w, L0_xattn_out_b, L0_ffn_Wg,
           L0_ffn_W1, L0_ffn_W3, L0_ffn_W2, L0_ffn_Ws1, L0_ffn_Ws3, L0_ffn_Ws2):
    import concourse.bacc as bacc
    from concourse.bass_utils import run_bass_kernel_spmd

    f = lambda a: np.asarray(a)
    consts, halves = constants()

    def rows(a):
        full = np.zeros((P, a.shape[1]), np.float32)
        full[:a.shape[0]] = a
        return full

    latent = lambda a: f(a).T.reshape(2, P, L).transpose(1, 0, 2).reshape(P, 2 * L)
    consts.update({
        "gamma": latent(L0_xattn_ln_gamma), "beta": latent(L0_xattn_ln_beta),
        "gb": np.broadcast_to(np.tile(f(L0_xattn_g_b), 2), (P, 2 * L)),
        "thw": f(L0_xattn_theta_w).T, "phw": f(L0_xattn_phi_w).T, "gw": f(L0_xattn_g_w).T,
        "wg": f(L0_ffn_Wg).T.reshape(2, P, NE).transpose(1, 0, 2).reshape(P, 2 * NE),
        "outw": rows(np.concatenate([f(L0_xattn_out_w).T, f(L0_xattn_out_b).reshape(1, P)])),
        "thb": rows(f(L0_xattn_theta_b).reshape(L, 1)), "phb": rows(f(L0_xattn_phi_b).reshape(L, 1)),
    })
    params = np.concatenate([consts[n] for n in COLS], 1)
    assert params.shape == (P, NCOLS)

    w1 = np.concatenate([f(L0_ffn_Ws1).reshape(2, NF, T), f(L0_ffn_W1)])
    w3 = np.concatenate([f(L0_ffn_Ws3).reshape(2, NF, T), f(L0_ffn_W3)])
    w2 = np.concatenate([f(L0_ffn_Ws2).reshape(T, 2, NF).transpose(1, 0, 2), f(L0_ffn_W2)])
    w13 = np.concatenate([w1, w3], 1).transpose(0, 2, 1).reshape(NU, 2, P, UP1).transpose(0, 2, 1, 3).reshape(NU, P, 2 * UP1)
    w2 = w2.transpose(0, 2, 1).reshape(NU, 2, FC, T).transpose(0, 2, 1, 3).reshape(NU, FC, 2 * T)

    arrays = {"x_dram": f(x), "ctx_dram": f(ctx_2048), "params_dram": params, "halves_dram": halves,
              "w13_dram": w13, "w2_dram": w2}
    arrays = {n: np.ascontiguousarray(a) for n, a in arrays.items()}
    nc = bacc.Bacc("TRN2", target_bir_lowering=False, num_devices=1)
    args = [nc.dram_tensor(n, a.shape, mybir.dt.from_np(a.dtype), kind="ExternalInput").ap() for n, a in arrays.items()]
    out = nc.dram_tensor("out_dram", (B, P, T), F32, kind="ExternalOutput").ap()
    build(nc, *args, out)
    r = run_bass_kernel_spmd(nc, [arrays], core_ids=[0])
    return r.results[0]["out_dram"]
```
